# Optimizing a Trainium2 kernel written in Bass

```python
import numpy as np
import jax
import jax.numpy as jnp

def _softmax(x, axis=-1):
    return jax.nn.softmax(x, axis=axis)

def _gelu(x):
    return jax.nn.gelu(x, approximate=True)

def _silu(x):
    return jax.nn.silu(x)

def _sigmoid(x):
    return jax.nn.sigmoid(x)

def _layernorm(x, axis=-1, eps=1e-05):
    m = jnp.mean(x, axis=axis, keepdims=True)
    v = jnp.var(x, axis=axis, keepdims=True)
    return (x - m) / jnp.sqrt(v + eps)

def _scatter_add(tgt, idx, src, axis=0):
    return tgt.at[idx].add(src)

def _segment_sum(src, seg, n):
    return jax.ops.segment_sum(src, seg, n)
kernel_name = 'mk_gnn_resnorm_d1_gnn_r8_8303bb'

def setup_inputs(seed: int=0):
    np.random.seed(seed)
    _w = jnp.asarray

    def _rec_inputs():
        import jax
        import jax.numpy as jnp
        _gk = jax.random.key(seed)
        x = -0.000202 + 1 * jax.random.normal(jax.random.fold_in(_gk, 1), (12500, 128), jnp.float32)
        src = jax.random.randint(jax.random.fold_in(_gk, 2), (200000,), 0, 12500, jnp.int32)
        dst = jnp.minimum((12500 * jax.random.uniform(jax.random.fold_in(_gk, 3), (200000,)) ** 2.0).astype(jnp.int32), 99999)
        _o = jnp.argsort(dst, stable=True)
        src = src[_o]
        dst = dst[_o]
        edge_type_4 = jax.random.randint(jax.random.fold_in(_gk, 12), (200000,), 0, 4, jnp.int32)
        node_type_3 = jax.random.randint(jax.random.fold_in(_gk, 13), (12500,), 0, 3, jnp.int32)
        return (x, src, dst, edge_type_4, node_type_3)
    x, src, dst, edge_type_4, node_type_3 = _rec_inputs()

    def _L0_gnn_setup():
        import jax, jax.numpy as jnp
        import numpy as np
        N, E, IN, HID, H, DH, L, T, R = (6250, 100000, 128, 128, 4, 32, 2, 3, 4)

        def _typed_linear(x, W, b, node_type):
            out = jnp.zeros((x.shape[0], W.shape[-1]), x.dtype)
            for t in range(W.shape[0]):
                m = (node_type == t)[:, None]
                out = out + jnp.where(m, x @ W[t] + b[t], jnp.zeros((), x.dtype))
            return out

        def _segment_softmax(logits, seg, num_segments):
            mx = jax.ops.segment_max(logits, seg, num_segments=num_segments)
            ex = jnp.exp(logits - mx[seg])
            den = jax.ops.segment_sum(ex, seg, num_segments=num_segments)
            return ex / (den[seg] + 1e-16)

        def _hgt_layer(x, Wk, bk, Wq, bq, Wv, bv, Wa, ba, a_rel, m_rel, mu, skip, node_type, src, dst, edge_type):
            n = x.shape[0]
            k = _typed_linear(x, Wk, bk, node_type).reshape(n, H, DH)
            q = _typed_linear(x, Wq, bq, node_type).reshape(n, H, DH)
            v = _typed_linear(x, Wv, bv, node_type).reshape(n, H, DH)
            kt = jnp.einsum('nhd,rhde->rnhe', k, a_rel)
            vt = jnp.einsum('nhd,rhde->rnhe', v, m_rel)
            k_e = kt[edge_type, src]
            v_e = vt[edge_type, src]
            att = (q[dst] * k_e).sum(-1) * mu[edge_type] / np.sqrt(DH)
            alpha = _segment_softmax(att, dst, n)
            agg = jax.ops.segment_sum(v_e * alpha[..., None], dst, num_segments=n).reshape(n, H * DH)
            out = _typed_linear(jax.nn.gelu(agg), Wa, ba, node_type)
            a = jax.nn.sigmoid(skip)[node_type][:, None]
            return a * out + (1.0 - a) * x
        key = jax.random.key(seed)
        k = jax.random.split(key, 16)
        s = 0.05
        return {'x': jax.random.normal(k[0], (N, IN), jnp.float32), 'W_in': jax.random.normal(k[1], (T, IN, HID)) * s, 'b_in': jnp.zeros((T, HID), jnp.float32), 'Wk': jax.random.normal(k[2], (L, T, HID, HID)) * s, 'bk': jnp.zeros((L, T, HID), jnp.float32), 'Wq': jax.random.normal(k[3], (L, T, HID, HID)) * s, 'bq': jnp.zeros((L, T, HID), jnp.float32), 'Wv': jax.random.normal(k[4], (L, T, HID, HID)) * s, 'bv': jnp.zeros((L, T, HID), jnp.float32), 'Wa': jax.random.normal(k[5], (L, T, HID, HID)) * s, 'ba': jnp.zeros((L, T, HID), jnp.float32), 'a_rel': jax.random.normal(k[6], (L, R, H, DH, DH)) * 0.1, 'm_rel': jax.random.normal(k[7], (L, R, H, DH, DH)) * 0.1, 'mu': jnp.ones((L, R, H), jnp.float32), 'skip': jnp.ones((L, T), jnp.float32), 'node_type': jax.random.randint(k[8], (N,), 0, T), 'edge_index': jax.random.randint(k[9], (2, E), 0, N), 'edge_type': jax.random.randint(k[10], (E,), 0, R)}
    _L0_gnn_all = _L0_gnn_setup()
    _L0_gnn_in = {k: v for k, v in _L0_gnn_all.items() if k in ('W_in', 'b_in', 'Wk', 'bk', 'Wq', 'bq', 'Wv', 'bv', 'Wa', 'ba', 'a_rel', 'm_rel', 'mu', 'skip')}
    del _L0_gnn_all
    return {'x': x, 'src': src, 'dst': dst, 'edge_type_4': edge_type_4, 'node_type_3': node_type_3, 'L0_gnn_W_in': _L0_gnn_in['W_in'], 'L0_gnn_b_in': _L0_gnn_in['b_in'], 'L0_gnn_Wk': _L0_gnn_in['Wk'], 'L0_gnn_bk': _L0_gnn_in['bk'], 'L0_gnn_Wq': _L0_gnn_in['Wq'], 'L0_gnn_bq': _L0_gnn_in['bq'], 'L0_gnn_Wv': _L0_gnn_in['Wv'], 'L0_gnn_bv': _L0_gnn_in['bv'], 'L0_gnn_Wa': _L0_gnn_in['Wa'], 'L0_gnn_ba': _L0_gnn_in['ba'], 'L0_gnn_a_rel': _L0_gnn_in['a_rel'], 'L0_gnn_m_rel': _L0_gnn_in['m_rel'], 'L0_gnn_mu': _L0_gnn_in['mu'], 'L0_gnn_skip': _L0_gnn_in['skip']}

def reference(x, src, dst, edge_type_4, node_type_3, L0_gnn_W_in, L0_gnn_b_in, L0_gnn_Wk, L0_gnn_bk, L0_gnn_Wq, L0_gnn_bq, L0_gnn_Wv, L0_gnn_bv, L0_gnn_Wa, L0_gnn_ba, L0_gnn_a_rel, L0_gnn_m_rel, L0_gnn_mu, L0_gnn_skip):
    import jax
    import jax.numpy as jnp

    def _L0_gnn_ref(x, W_in, b_in, Wk, bk, Wq, bq, Wv, bv, Wa, ba, a_rel, m_rel, mu, skip, node_type, edge_index, edge_type):
        import jax, jax.numpy as jnp
        import numpy as np
        N, E, IN, HID, H, DH, L, T, R = (6250, 100000, 128, 128, 4, 32, 2, 3, 4)

        def _typed_linear(x, W, b, node_type):
            out = jnp.zeros((x.shape[0], W.shape[-1]), x.dtype)
            for t in range(W.shape[0]):
                m = (node_type == t)[:, None]
                out = out + jnp.where(m, x @ W[t] + b[t], jnp.zeros((), x.dtype))
            return out

        def _segment_softmax(logits, seg, num_segments):
            mx = jax.ops.segment_max(logits, seg, num_segments=num_segments)
            ex = jnp.exp(logits - mx[seg])
            den = jax.ops.segment_sum(ex, seg, num_segments=num_segments)
            return ex / (den[seg] + 1e-16)

        def _hgt_layer(x, Wk, bk, Wq, bq, Wv, bv, Wa, ba, a_rel, m_rel, mu, skip, node_type, src, dst, edge_type):
            n = x.shape[0]
            k = _typed_linear(x, Wk, bk, node_type).reshape(n, H, DH)
            q = _typed_linear(x, Wq, bq, node_type).reshape(n, H, DH)
            v = _typed_linear(x, Wv, bv, node_type).reshape(n, H, DH)
            kt = jnp.einsum('nhd,rhde->rnhe', k, a_rel)
            vt = jnp.einsum('nhd,rhde->rnhe', v, m_rel)
            k_e = kt[edge_type, src]
            v_e = vt[edge_type, src]
            att = (q[dst] * k_e).sum(-1) * mu[edge_type] / np.sqrt(DH)
            alpha = _segment_softmax(att, dst, n)
            agg = jax.ops.segment_sum(v_e * alpha[..., None], dst, num_segments=n).reshape(n, H * DH)
            out = _typed_linear(jax.nn.gelu(agg), Wa, ba, node_type)
            a = jax.nn.sigmoid(skip)[node_type][:, None]
            return a * out + (1.0 - a) * x
        src, dst = (edge_index[0], edge_index[1])
        h = _typed_linear(x, W_in, b_in, node_type)
        for l in range(L):
            h = _hgt_layer(h, Wk[l], bk[l], Wq[l], bq[l], Wv[l], bv[l], Wa[l], ba[l], a_rel[l], m_rel[l], mu[l], skip[l], node_type, src, dst, edge_type)
        return h
    edge_index = jnp.stack([src, dst])
    x = _layernorm(x + _L0_gnn_ref(x, L0_gnn_W_in, L0_gnn_b_in, L0_gnn_Wk, L0_gnn_bk, L0_gnn_Wq, L0_gnn_bq, L0_gnn_Wv, L0_gnn_bv, L0_gnn_Wa, L0_gnn_ba, L0_gnn_a_rel, L0_gnn_m_rel, L0_gnn_mu, L0_gnn_skip, node_type_3, edge_index, edge_type_4), axis=-1)
    return x

_drawn_inputs = setup_inputs


def setup_inputs(seed=0):
    import zlib

    import numpy as np

    out = dict(_drawn_inputs(seed))
    spreads = {'L0_gnn_b_in': (0.0, 0.8),
     'L0_gnn_bk': (0.0, 0.8),
     'L0_gnn_bq': (0.0, 0.8),
     'L0_gnn_bv': (0.0, 0.8),
     'L0_gnn_ba': (0.0, 0.1),
     'L0_gnn_mu': (1.0, 0.6),
     'L0_gnn_skip': (1.0, 0.6)}
    factors = {'L0_gnn_Wk': 8.0,
     'L0_gnn_Wq': 8.0,
     'L0_gnn_Wv': 8.0,
     'L0_gnn_Wa': 8.0,
     'L0_gnn_a_rel': 8.0,
     'L0_gnn_m_rel': 8.0}
    for name, (base, spread) in spreads.items():
        noise = np.random.default_rng([zlib.crc32(name.encode()), seed]).standard_normal(out[name].shape)
        drawn = base * np.exp(spread * noise) if base else spread * noise
        out[name] = jnp.asarray(drawn.astype(out[name].dtype))
    for name, factor in factors.items():
        out[name] = (out[name] * factor).astype(out[name].dtype)
    return out
```

```python
from contextlib import ExitStack

import concourse.bass as bass
from concourse import mybir

F32 = mybir.dt.float32
BF16 = mybir.dt.bfloat16
I32 = mybir.dt.int32
ALU = mybir.AluOpType
ACT = mybir.ActivationFunctionType
AX = mybir.AxisListType

N, E, D = 12500, 200000, 128
H, DH, LAYERS, TYPES, RELS = 4, 32, 2, 3, 4
P = 128
TILES = -(-N // P)
NP = TILES * P
SPB, SPG = 32, 4
GPB = SPB // SPG
BLOCKS = -(-(E // P + TILES) // SPB)
STEPS = BLOCKS * SPB
SK = STEPS // P
EPAD = SK * P * P
EP, EF = 125, E // 125
HW = DH + 1
AW = H * HW
SLOTS = 3
BANK = 512
BIG = 1e38
EPS = 1e-5
FAR = 20000.0
WHY = "computed on the chip from the step number and clamped by construction"


class Phase:

    def __init__(self, nc, tag):
        self.nc, self.tag, self.stack = nc, tag, ExitStack()
        self.semaphores = []
        self.stack.callback(self.clear_semaphores)

    def clear_semaphores(self):
        if self.semaphores:
            self.nc.clear_and_free_semaphores(self.semaphores)
            self.nc.all_engine_barrier()

    def sb(self, name, shape, dtype=F32):
        return self.stack.enter_context(self.nc.sbuf_tensor(f"{self.tag}_{name}", shape, dtype))

    def ps(self, name, shape, dtype=F32):
        return self.stack.enter_context(self.nc.psum_tensor(f"{self.tag}_{name}", shape, dtype))

    def sem(self, name):
        self.semaphores.append(self.nc.alloc_semaphore(f"{self.tag}_{name}"))
        return self.semaphores[-1]


def dram_ap(ap, offset, pattern):
    return bass.AP(tensor=ap.tensor, offset=offset, ap=pattern)


def edge_plan(nc, dram, const):
    ph = Phase(nc, "plan")
    with ph.stack:
        sb, sem = ph.sb, ph.sem
        src_i, et_i, dst_i = (sb(n, [EP, EF], I32) for n in ("src_i", "et_i", "dst_i"))
        row_f, dst_f = sb("row_f", [EP, EF]), sb("dst_f", [EP, EF])
        TW = 112
        TP = (EPAD - E) // TW
        tail_row, tail_dst = sb("tail_row", [TP, TW]), sb("tail_dst", [TP, TW])
        type_i, type_f = sb("type_i", [100, N // 100], I32), sb("type_f", [100, N // 100])
        zeros = sb("zeros", [1, P])
        last = sb("last", [P, SK])
        tile_i, tile_id = sb("tile_i", [P, TILES], I32), sb("tile_id", [P, TILES])
        tile_start = sb("tile_start", [P, TILES])
        column_i = sb("column_i", [P, P], I32)
        step_i, step_f = sb("step_i", [P, SK], I32), sb("step_f", [P, SK])
        compare = sb("compare", [P, SK, TILES])
        chunks_before = sb("chunks_before", [P, TILES])
        first_step = sb("first_step", [P, TILES])
        tile_of, tile_base, is_first = sb("tile_of", [P, SK]), sb("tile_base", [P, SK]), sb("is_first", [P, SK])
        chunk_i = sb("chunk_i", [P, SK], I32)
        tile_slot_i, tile_slot = sb("tile_slot_i", [P, -(-TILES // SLOTS) * SLOTS], I32), sb("tile_slot", [P, -(-TILES // SLOTS) * SLOTS])
        slot_of, slot_wrap, info = sb("slot_of", [P, SK]), sb("slot_wrap", [P, SK]), sb("info", [P, 5, SK], I32)
        rows, dsts = sb("rows", [P, SK, P]), sb("dsts", [P, SK, P])
        local, inside, key = sb("local", [P, SK, P]), sb("inside", [P, SK, P]), sb("key", [P, SK, P])
        before, link = sb("before", [P, SK, P]), sb("link", [P, SK, P])
        whole, link_next = sb("whole", [P, SK]), sb("link_next", [P, SK])
        run_fwd, run_bwd = sb("run_fwd", [P, SK]), sb("run_bwd", [P, SK])
        big_row = sb("big_row", [1, P])
        rows_t, local_t = sb("rows_t", [P, STEPS], I32), sb("local_t", [P, STEPS], BF16)
        count_ps = ph.ps("count_ps", [P, TILES])
        turn_ps = ph.ps("turn_ps", [P, 2, BANK])
        s_load, s_type, s_flat, s_last = sem("s_load"), sem("s_type"), sem("s_flat"), sem("s_last")
        s_set, s_io, s_v, s_cnt, s_gather = sem("s_set"), sem("s_io"), sem("s_v"), sem("s_cnt"), sem("s_gather")
        s_key, s_before, s_link, s_next, s_t, s_tc, s_out = (
            sem(n) for n in ("s_key", "s_before", "s_link", "s_next", "s_t", "s_tc", "s_out"))
        mark = {}

        def by_step(ap):
            return ap.rearrange("(k p) -> p k", p=P)

        with nc.Block() as block:
            @block.vector
            def _(dve):
                count = [0]

                def then(instruction):
                    count[0] += 1
                    instruction.then_inc(s_v, 1)
                    dve.wait_ge(s_v, count[0])

                dve.wait_ge(s_load, 48)
                dve.wait_ge(s_type, 16)
                then(dve.scalar_tensor_tensor(out=row_f[:, :], in0=et_i[:, :], scalar=float(NP), in1=src_i[:, :], op0=ALU.mult, op1=ALU.add))
                then(dve.tensor_copy(dst_f[:, :], dst_i[:, :]))
                then(dve.tensor_copy(type_f[:, :], type_i[:, :]))
                mark["flat"] = count[0]
                dve.wait_ge(s_io, 5)
                then(dve.tensor_copy(tile_id[:, :], tile_i[:, :]))
                then(dve.tensor_copy(step_f[:, :], step_i[:, :]))
                then(dve.tensor_copy(tile_slot[:, :], tile_slot_i[:, :]))
                then(dve.tensor_copy(const["column16"][:, :], column_i[:, :]))
                then(dve.tensor_copy(const["row"][:, :], const["row_i"][:, :]))
                then(dve.tensor_scalar(tile_start[:, :], tile_id[:, :], float(P), None, ALU.mult))
                dve.wait_ge(s_set, 8)
                then(dve.tensor_copy(const["ident16"][:, :], const["ident"][:, :]))
                dve.wait_ge(s_last, 16)
                wide = [P, SK, TILES]
                then(dve.tensor_tensor(compare[:, :, :], last[:, :].unsqueeze(2).broadcast_to(wide),
                                               tile_start[:, :].unsqueeze(1).broadcast_to(wide), ALU.is_lt))
                then(dve.tensor_reduce(chunks_before[:, :], compare[:, :, :].rearrange("p k t -> p t k"), AX.X, ALU.add))
                mark["count"] = count[0]
                dve.wait_ge(s_cnt, 1)
                then(dve.tensor_tensor(first_step[:, :], count_ps[:, :], tile_id[:, :], ALU.add))
                by_tile = lambda: (first_step[:, :].unsqueeze(1).broadcast_to(wide), step_f[:, :].unsqueeze(2).broadcast_to(wide))
                then(dve.tensor_tensor(compare[:, :, :], *by_tile(), ALU.is_le))
                then(dve.tensor_reduce(tile_of[:, :], compare[:, :, :], AX.X, ALU.add))
                then(dve.tensor_tensor(compare[:, :, :], *by_tile(), ALU.is_equal))
                then(dve.tensor_reduce(is_first[:, :], compare[:, :, :], AX.X, ALU.add))
                then(dve.tensor_scalar(tile_of[:, :], tile_of[:, :], -1.0, None, ALU.add))
                then(dve.tensor_tensor(chunk_i[:, :], step_f[:, :], tile_of[:, :], ALU.subtract))
                mark["chunk"] = count[0]
                then(dve.tensor_scalar(tile_base[:, :], tile_of[:, :], float(P), None, ALU.mult))
                then(dve.tensor_tensor(compare[:, :, :], tile_of[:, :].unsqueeze(2).broadcast_to(wide),
                                       tile_id[:, :].unsqueeze(1).broadcast_to(wide), ALU.is_equal))
                then(dve.tensor_tensor(compare[:, :, :], compare[:, :, :], tile_slot[:, 0:TILES].unsqueeze(1).broadcast_to(wide), ALU.mult))
                then(dve.tensor_reduce(slot_of[:, :], compare[:, :, :], AX.X, ALU.add))
                then(dve.tensor_copy(info[:, 0, :], tile_base[:, :]))
                then(dve.tensor_scalar(info[:, 1, :], slot_of[:, :], float(BANK), None, ALU.mult))
                then(dve.scalar_tensor_tensor(out=is_first[:, :], in0=slot_of[:, :], scalar=-float(SLOTS), in1=is_first[:, :],
                                              op0=ALU.add, op1=ALU.mult))
                then(dve.tensor_scalar(info[:, 2, :], is_first[:, :], float(BANK), float(SLOTS * BANK), ALU.mult, ALU.add))
                then(dve.tensor_scalar(slot_wrap[:, :], slot_of[:, :], 1.0, -float(SLOTS), ALU.is_ge, ALU.mult))
                then(dve.tensor_tensor(slot_wrap[:, :], slot_wrap[:, :], slot_of[:, :], ALU.add))
                then(dve.tensor_scalar(info[:, 3, :], slot_wrap[:, :], float(BANK), float((SLOTS - 1) * BANK), ALU.mult, ALU.add))
                then(dve.tensor_scalar(info[:, 4, :], tile_of[:, :], float(AW), None, ALU.mult))
                dve.wait_ge(s_gather, 16 * 2 * SK)
                full = [P, SK, P]
                then(dve.tensor_tensor(local[:, :, :], dsts[:, :, :], tile_base[:, :].unsqueeze(2).broadcast_to(full), ALU.subtract))
                then(dve.tensor_scalar(local[:, :, :], local[:, :, :], -1.0, float(P), ALU.max, ALU.min))
                then(dve.tensor_scalar(inside[:, :, :], local[:, :, :], 0.0, float(P - 1), ALU.max, ALU.min))
                then(dve.tensor_tensor(inside[:, :, :], inside[:, :, :], local[:, :, :], ALU.is_equal))
                then(dve.scalar_tensor_tensor(out=key[:, :, :], in0=dsts[:, :, :], scalar=1.0, in1=inside[:, :, :], op0=ALU.add, op1=ALU.mult))
                mark["key"] = count[0]
                dve.wait_ge(s_before, 16)
                then(dve.tensor_tensor(link[:, :, :], key[:, :, :], before[:, :, :], ALU.is_equal))
                then(dve.scalar_tensor_tensor(out=link[:, :, :], in0=key[:, :, :], scalar=0.0, in1=link[:, :, :], op0=ALU.is_gt, op1=ALU.mult))
                then(dve.tensor_scalar(link[:, :, :], link[:, :, :], -1.0, BIG, ALU.add, ALU.mult))
                mark["link"] = count[0]
                then(dve.tensor_reduce(whole[:, :], link[:, :, 1:P], AX.X, ALU.min))
                then(dve.tensor_tensor(run_fwd[:, :], whole[:, :], link[:, :, 0], ALU.min))
                dve.wait_ge(s_next, 16)
                then(dve.tensor_tensor(run_bwd[:, :], whole[:, :], link_next[:, :], ALU.min))
                mark["runs"] = count[0]
                for k in range(SK):
                    for m, out in ((0, rows_t), (1, local_t)):
                        dve.wait_ge(s_t, 2 * k + m + 1)
                        dve.tensor_copy(out[:, k * P:(k + 1) * P], turn_ps[:, m, 0:P]).then_inc(s_tc, 1)

            @block.gpsimd
            def _(pool):
                pool.memset(const["ident"][:, :], 0.0).then_inc(s_set, 1)
                pool.memset(const["ones"][:, :], 1.0).then_inc(s_set, 1)
                pool.memset(const["zero16"][:, :], 0.0).then_inc(s_set, 1)
                pool.memset(zeros[:, :], 0.0).then_inc(s_set, 1)
                pool.memset(big_row[:, :], -BIG).then_inc(s_set, 1)
                pool.memset(tail_row[:, :], 0.0).then_inc(s_set, 1)
                pool.memset(tail_dst[:, :], FAR).then_inc(s_set, 1)
                pool.iota(tile_i[:, :], [[1, TILES]], base=0, channel_multiplier=0).then_inc(s_io, 1)
                pool.iota(tile_slot_i[:, :], [[0, -(-TILES // SLOTS)], [1, SLOTS]], base=0, channel_multiplier=0).then_inc(s_io, 1)
                pool.iota(step_i[:, :], [[P, SK]], base=0, channel_multiplier=1).then_inc(s_io, 1)
                pool.iota(column_i[:, :], [[1, P]], base=0, channel_multiplier=0).then_inc(s_io, 1)
                pool.iota(const["row_i"][:, :], [[1, 1]], base=0, channel_multiplier=1).then_inc(s_io, 1)
                pool.memset(const["sums"][:, TILES + 1, :], 0.0)
                pool.wait_ge(s_set, 7)
                pool.affine_select(out=const["ident"][:, :], in_=const["ident"][:, :], compare_op=ALU.not_equal,
                                   fill=1.0, base=0, pattern=[[-1, P]], channel_multiplier=1).then_inc(s_set, 1)
                pool.wait_ge(s_flat, 64)
                pool.wait_ge(s_v, mark["chunk"])
                for k in range(SK):
                    for to, table in ((rows, dram["edge_row"]), (dsts, dram["edge_dst"])):
                        pool.indirect_dma_start(
                            to[:, k, :], None, table,
                            bass.IndirectOffsetOnAxis(ap=chunk_i[:, k:k + 1], axis=0)).then_inc(s_gather, 16)

            @block.sync
            def _(sp):
                for to, name in ((src_i, "src"), (et_i, "edge_type"), (dst_i, "dst")):
                    sp.dma_start(to[:, :], dram[name].rearrange("(p n) -> p n", p=EP)).then_inc(s_load, 16)
                sp.dma_start(type_i[:, :], dram["node_type"].rearrange("(p n) -> p n", p=100)).then_inc(s_type, 16)
                sp.wait_ge(s_set, 8)
                sp.dma_start(dram["edge_row_flat"][E:EPAD].rearrange("(p n) -> p n", p=TP), tail_row[:, :]).then_inc(s_flat, 16)
                sp.dma_start(dram["edge_dst_flat"][E:EPAD].rearrange("(p n) -> p n", p=TP), tail_dst[:, :]).then_inc(s_flat, 16)
                sp.dma_start(dram["type_f"][N:NP].unsqueeze(0), zeros[:, 0:NP - N]).then_inc(s_out, 16)
                sp.dma_start(dram["key"][0:1].unsqueeze(0), zeros[:, 0:1]).then_inc(s_key, 16)
                sp.dma_start(dram["link"][STEPS * P:(STEPS + 1) * P].unsqueeze(0), big_row[:, :]).then_inc(s_link, 16)
                sp.wait_ge(s_v, mark["flat"])
                sp.dma_start(dram["edge_row_flat"][0:E].rearrange("(p n) -> p n", p=EP), row_f[:, :]).then_inc(s_flat, 16)
                sp.dma_start(dram["edge_dst_flat"][0:E].rearrange("(p n) -> p n", p=EP), dst_f[:, :]).then_inc(s_flat, 16)
                sp.dma_start(dram["type_f"][0:N].rearrange("(p n) -> p n", p=100), type_f[:, :]).then_inc(s_out, 16)
                sp.wait_ge(s_flat, 64)
                sp.dma_start(last[:, :], by_step(dram["edge_dst"][:, P - 1]), allow_slow_non_contiguous=True).then_inc(s_last, 16)
                sp.wait_ge(s_v, mark["key"])
                sp.dma_start(dram["key"][1:1 + STEPS * P].rearrange("(k p e) -> p k e", p=P, e=P), key[:, :, :]).then_inc(s_key, 16)
                sp.wait_ge(s_key, 32)
                sp.dma_start(before[:, :, :], dram["key"][0:STEPS * P].rearrange("(k p e) -> p k e", p=P, e=P)).then_inc(s_before, 16)
                sp.wait_ge(s_v, mark["link"])
                sp.dma_start(dram["link"][0:STEPS * P].rearrange("(k p e) -> p k e", p=P, e=P), link[:, :, :]).then_inc(s_link, 16)
                sp.wait_ge(s_link, 32)
                sp.dma_start(link_next[:, :], dram_ap(dram["link"], P, [[P, P], [P * P, SK]]),
                             allow_slow_non_contiguous=True).then_inc(s_next, 16)
                sp.wait_ge(s_v, mark["runs"])
                sp.dma_start(by_step(dram["run_fwd"]), run_fwd[:, :], allow_slow_non_contiguous=True).then_inc(s_out, 16)
                sp.dma_start(by_step(dram["run_bwd"]), run_bwd[:, :], allow_slow_non_contiguous=True).then_inc(s_out, 16)
                for c in range(5):
                    sp.dma_start(by_step(dram["info"][c, :]), info[:, c, :], allow_slow_non_contiguous=True).then_inc(s_out, 16)
                sp.wait_ge(s_tc, 2 * SK)
                sp.dma_start(dram["rows_t"], rows_t[:, :]).then_inc(s_out, 16)
                sp.dma_start(dram["local_t"], local_t[:, :]).then_inc(s_out, 16)
                sp.wait_ge(s_out, 16 * 11)

            @block.tensor
            def _(pe):
                pe.wait_ge(s_set, 8)
                pe.wait_ge(s_v, mark["count"])
                pe.matmul(count_ps[:, :], const["ones"][:, :], chunks_before[:, :], start=True, stop=True).then_inc(s_cnt, 1)
                pe.wait_ge(s_gather, 16 * 2 * SK)
                pe.wait_ge(s_v, mark["key"])
                for k in range(SK):
                    for m, what in ((0, rows), (1, local)):
                        if k:
                            pe.wait_ge(s_tc, 2 * (k - 1) + m + 1)
                        pe.transpose(turn_ps[:, m, 0:P], what[:, k, :], const["ident"][:, :]).then_inc(s_t, 1)



def at_least(engine, semaphore, value):
    if not isinstance(value, int) or value > 0:
        engine.wait_ge(semaphore, value)


def node_phase(nc, dram, const, layer):
    from_x, ends = layer == 0, layer == LAYERS
    ph = Phase(nc, f"node{layer}")
    with ph.stack:
        sb, ps, sem = ph.sb, ph.ps, ph.sem
        q, sums = const["q"], const["sums"]
        w1, b1 = sb("w1", [P, TYPES, P]), sb("b1", [TYPES, P])
        if not from_x:
            skip_all, skip_col, stay = sb("skip_all", [P, TYPES]), sb("skip_col", [TYPES, 1]), sb("stay", [TYPES, P])
            weight, recip = sb("weight", [P, H]), sb("recip", [P, 2, H])
            mean_v, g = sb("mean_v", [P, 2, P]), sb("g", [P, 2, P])
            h_old, stayed = sb("h_old", [P, 2, P]), sb("stayed", [P, P])
        if not ends:
            wq, wk, wv = (sb(n, [P, TYPES, P]) for n in ("wq", "wk", "wv"))
            bq, bk, bv = (sb(n, [TYPES, P]) for n in ("bq", "bk", "bv"))
            ak, am = sb("ak", [P, RELS, P]), sb("am", [P, RELS, P])
            mu = sb("mu", [P, RELS * H])
            h_typed, kv_t = sb("h_typed", [P, TYPES, P]), sb("kv_t", [P, 2 * P])
            table = sb("table", [P, 2, RELS, 2 * P])
        else:
            summed, stats, moment = sb("summed", [P, P]), sb("stats", [P, 6]), sb("moment", [P, 2])
            moments = sb("moments", [P, TILES, 2])
            spread, rstd = sb("spread", [P, TILES]), sb("rstd", [P, TILES])
        x = sb("x", [P, 2, P])
        types, types3, onehot = sb("types", [P, 2, P]), sb("types3", [TYPES, 2, P]), sb("onehot", [TYPES, 2, P])
        in_typed, h = sb("in_typed", [P, TYPES, P]), sb("h", [P, 2, P])
        in_ps, h_ps, qkv_ps = ps("in_ps", [P, BANK]), ps("h_ps", [P, BANK]), ps("qkv_ps", [P, BANK])
        k_ps, v_ps = ps("k_ps", [P, BANK]), ps("v_ps", [P, BANK])
        s_w, s_wv, s_ws, s_z, s_chain, s_out, s_pause, s_aggr = (
            sem(n) for n in ("s_w", "s_wv", "s_ws", "s_z", "s_chain", "s_out", "s_pause", "s_aggr"))
        s_in, s_hst, s_tst = ([sem(f"{n}{u}") for u in range(2)] for n in ("s_in", "s_hst", "s_tst"))
        s_mean, s_g, s_x, s_it, s_h, s_stay, s_hs, s_ht = (
            sem(n) for n in ("s_mean", "s_g", "s_x", "s_it", "s_h", "s_stay", "s_hs", "s_ht"))
        s_qkv, s_kv, s_tab, s_tk, s_tv, s_y, s_norm = (
            sem(n) for n in ("s_qkv", "s_kv", "s_tab", "s_tk", "s_tv", "s_y", "s_norm"))
        mark = {}
        loads = 3 if from_x or not ends else 4
        table_out = None if ends else dram["table"][layer].rearrange("(r n) c -> n r c", r=RELS)

        def over_tiles(engine, turn):
            turn((0, 0, 0), None)
            for i in (1, 2, 3):
                turn((i, i % 2, i // 2), (i - 1, (i - 1) % 2, (i - 1) // 2))
            with engine.Fori(2, TILES // 2) as k:
                turn((k * 2, 0, k), (k * 2 - 1, 1, k - 1))
                turn((k * 2 + 1, 1, k), (k * 2, 0, k))
            turn(None, (TILES - 1, 1, TILES // 2 - 1))

        def is_tile(i, number):
            return isinstance(i, int) and i == number

        with nc.Block() as block:
            @block.vector
            def _(dve):
                count = [0]

                def then(instruction):
                    count[0] += 1
                    instruction.then_inc(s_wv, 1)
                    dve.wait_ge(s_wv, count[0])

                if not ends:
                    then(dve.memset(ak[:, :, :], 0.0))
                    then(dve.memset(am[:, :, :], 0.0))
                    mark["cleared"] = count[0]
                dve.wait_ge(s_w, mark_loads(from_x, ends))
                if not ends:
                    blocks = [P, RELS * H, DH]
                    flat = ak[:, :, :].rearrange("p r (h e) -> p (r h) e", e=DH)
                    then(dve.scalar_tensor_tensor(out=flat, in0=flat, scalar=float(DH) ** -0.5, op0=ALU.mult,
                                                  in1=mu[:, :].unsqueeze(2).broadcast_to(blocks), op1=ALU.mult))
                if not from_x:
                    dve.wait_ge(s_ws, 1)
                    for t in range(TYPES):
                        then(dve.tensor_scalar(w1[:, t, :], w1[:, t, :], skip_all[:, t:t + 1], None, ALU.mult))
                    then(dve.tensor_scalar(b1[:, :], b1[:, :], skip_col[:, :], None, ALU.mult))
                    then(dve.tensor_scalar(stay[:, :], const["ones"][0:TYPES, :], skip_col[:, :], None, ALU.mult))
                    then(dve.tensor_scalar(stay[:, :], stay[:, :], -1.0, 1.0, ALU.mult, ALU.add))
                mark["weights"] = count[0]
                def mean(i, u):
                    at_least(dve, s_g, i - 1)
                    one = sums[:, bass.ds(i + 1, 1), :].rearrange("p o (h c) -> p (o h) c", c=HW)
                    dve.tensor_scalar(weight[:, :], one[:, :, DH], 1e-16, None, ALU.add).then_inc(s_chain, 1)
                    dve.wait_ge(s_chain, i * 2 + 1)
                    dve.reciprocal(recip[:, u, :], weight[:, :]).then_inc(s_chain, 1)
                    dve.wait_ge(s_chain, i * 2 + 2)
                    dve.tensor_tensor(mean_v[:, u, :].rearrange("p (h c) -> p h c", c=DH), one[:, :, 0:DH],
                                      recip[:, u, :].unsqueeze(2).broadcast_to([P, H, DH]), ALU.mult).then_inc(s_mean, 1)

                def first_half(i, u, k):
                    if is_tile(i, 0) and not from_x:
                        mean(0, 0)
                    dve.wait_ge(s_in[u], (k + 1) * (16 * loads))
                    dve.wait_ge(s_x, i + 1)
                    at_least(dve, s_h, i)
                    at_least(dve, s_qkv if not ends else s_h, i - 1)
                    for t in range(TYPES):
                        dve.scalar_tensor_tensor(out=in_typed[:, t, :], in0=types[:, u, :], scalar=float(t),
                                                 in1=in_ps[:, 0:P], op0=ALU.is_equal, op1=ALU.mult)
                    dve.tensor_scalar(onehot[:, u, :], types3[:, u, :], const["row"][0:TYPES, :], None,
                                      ALU.is_equal).then_inc(s_it, 1)
                    if not from_x:
                        dve.wait_ge(s_h, i + 1)
                        at_least(dve, s_hs, i)
                        dve.tensor_tensor(stayed[:, :], h_ps[:, P:2 * P], h_old[:, u, :], ALU.mult).then_inc(s_stay, 1)
                        dve.wait_ge(s_stay, i + 1)
                        at_least(dve, s_y if ends else s_ht, i - 1)
                        if not ends:
                            at_least(dve, s_hst[u], k * 16)
                        dve.tensor_tensor(h[:, u, :], stayed[:, :], h_ps[:, 0:P], ALU.add).then_inc(s_hs, 1)
                    if not ends:
                        dve.wait_ge(s_hs, i + 1)
                        at_least(dve, s_qkv, i)
                        for t in range(TYPES):
                            last = dve.scalar_tensor_tensor(out=h_typed[:, t, :], in0=types[:, u, :], scalar=float(t),
                                                            in1=h[:, u, :], op0=ALU.is_equal, op1=ALU.mult)
                        last.then_inc(s_ht, 1)
                    if not from_x:
                        mean(i + 1, 1 - u)

                def second_half(i, u, k):
                    if ends:
                        dve.wait_ge(s_y, i + 1)
                        at_least(dve, s_norm, i * 4)
                        dve.tensor_tensor(summed[:, :], k_ps[:, 0:P], x[:, u, :], ALU.add).then_inc(s_norm, 1)
                        dve.wait_ge(s_norm, i * 4 + 1)
                        dve.tensor_copy(q[:, bass.ds(i, 1), :].rearrange("p o c -> p (o c)"), summed[:, :]).then_inc(s_norm, 1)
                        dve.bn_stats(stats[:, :], summed[:, :]).then_inc(s_norm, 1)
                        dve.wait_ge(s_norm, i * 4 + 3)
                        dve.sem_inc(s_pause, 1)
                        dve.bn_aggr(moment[:, :], stats[:, :]).then_inc(s_aggr, 1)
                        dve.wait_ge(s_aggr, i + 1)
                        dve.tensor_copy(moments[:, bass.ds(i, 1), :].rearrange("p o c -> p (o c)"), moment[:, :]).then_inc(s_norm, 1)
                        return
                    dve.wait_ge(s_tab, i + 1)
                    at_least(dve, s_tst[u], k * 16)
                    dve.tensor_copy(table[:, u, :, 0:P], k_ps[:, :].rearrange("p (r c) -> p r c", c=P)).then_inc(s_tk, 1)

                def turn(new, old):
                    if new:
                        first_half(*new)
                    if old:
                        second_half(*old)

                over_tiles(dve, turn)
                if ends:
                    done = TILES * 4
                    dve.wait_ge(s_norm, done)
                    dve.tensor_scalar(spread[:, :], moments[:, :, 1], EPS, None, ALU.add).then_inc(s_norm, 1)
                    dve.wait_ge(s_z, 1)
                    dve.reciprocal(rstd[:, :], rstd[:, :]).then_inc(s_norm, 1)
                    dve.wait_ge(s_norm, done + 2)
                    with dve.Fori(0, TILES) as i:
                        one = q[:, bass.ds(i, 1), :].rearrange("p o c -> p (o c)")
                        dve.tensor_scalar(one, one, moments[:, bass.ds(i, 1), 0:1].rearrange("p o c -> p (o c)"),
                                          rstd[:, bass.ds(i, 1)], ALU.subtract, ALU.mult).then_inc(s_norm, 1)

            @block.scalar
            def _(act):
                if not from_x:
                    act.wait_ge(s_w, mark_loads(from_x, ends))
                    act.activation(skip_all[:, :], skip_all[:, :], ACT.Sigmoid)
                    act.activation(skip_col[:, :], skip_col[:, :], ACT.Sigmoid).then_inc(s_ws, 1)

                def gelu(i, u):
                    act.wait_ge(s_mean, i + 1)
                    at_least(act, s_x, i - 1)
                    act.activation(g[:, u, :], mean_v[:, u, :], ACT.Gelu_apprx_tanh).then_inc(s_g, 1)

                def turn(new, old):
                    if old and not ends:
                        i, u, k = old
                        act.wait_ge(s_qkv, i + 1)
                        act.activation(q[:, bass.ds(i, 1), :].rearrange("p o c -> p (o c)"), qkv_ps[:, 0:P], ACT.Copy)
                        at_least(act, s_tab, i)
                        act.activation(kv_t[:, :], qkv_ps[:, P:3 * P], ACT.Copy).then_inc(s_kv, 1)
                    if new and from_x:
                        i, u, k = new
                        act.wait_ge(s_h, i + 1)
                        at_least(act, s_ht, i - 1)
                        at_least(act, s_hst[u], k * 16)
                        act.activation(h[:, u, :], h_ps[:, 0:P], ACT.Copy).then_inc(s_hs, 1)
                    if new and not from_x:
                        i, u, k = new
                        if is_tile(i, 0):
                            gelu(0, 0)
                        gelu(i + 1, 1 - u)
                    if old and not ends:
                        i, u, k = old
                        act.wait_ge(s_tab, i + 1)
                        at_least(act, s_tst[u], k * 16)
                        act.activation(table[:, u, :, P:2 * P], v_ps[:, :].rearrange("p (r c) -> p r c", c=P),
                                       ACT.Copy).then_inc(s_tv, 1)

                over_tiles(act, turn)
                if ends:
                    act.wait_ge(s_norm, TILES * 4 + 1)
                    act.activation(rstd[:, :], spread[:, :], ACT.Sqrt).then_inc(s_z, 1)

            @block.sync
            def _(sp):
                w_name, b_name = ("W_in", "b_in") if from_x else ("Wa", "ba")
                pick = (lambda name: dram[name]) if from_x else (lambda name: dram[name][layer - 1])
                to_in = lambda ap: ap.rearrange("t i o -> i t o")
                sp.dma_start(w1[:, :, :], to_in(pick(w_name))).then_inc(s_w, 16)
                sp.dma_start(b1[:, :], pick(b_name)).then_inc(s_w, 16)
                if not from_x:
                    skip = dram["skip"][layer - 1]
                    sp.dma_start(skip_all[:, :], skip.unsqueeze(0).broadcast_to([P, TYPES])).then_inc(s_w, 16)
                    sp.dma_start(skip_col[:, :], skip.unsqueeze(1), allow_slow_non_contiguous=True).then_inc(s_w, 16)
                if not ends:
                    for to, bias, name in ((wq, bq, "q"), (wk, bk, "k"), (wv, bv, "v")):
                        sp.dma_start(to[:, :, :], to_in(dram["W" + name][layer])).then_inc(s_w, 16)
                        sp.dma_start(bias[:, :], dram["b" + name][layer]).then_inc(s_w, 16)
                    sp.dma_start(mu[:, :], dram["mu"][layer].rearrange("r h -> (r h)").unsqueeze(0).broadcast_to(
                        [P, RELS * H])).then_inc(s_w, 16)
                    sp.wait_ge(s_wv, mark["cleared"])
                    for to, name in ((ak, "a_rel"), (am, "m_rel")):
                        for hd in range(H):
                            part = slice(hd * DH, (hd + 1) * DH)
                            sp.dma_start(to[part, :, part], dram[name][layer][:, hd, :, :].rearrange(
                                "r d e -> d r e")).then_inc(s_w, 16)

                def loads_of(i, u, k):
                    at_least(sp, s_norm if ends else s_ht, (i - 1) * 4 if ends else i - 1)
                    at = bass.ds(i * P, P)
                    row = dram["type_f"][at].unsqueeze(0)
                    sp.dma_start(types[:, u, :], row.broadcast_to([P, P])).then_inc(s_in[u], 16)
                    sp.dma_start(types3[:, u, :], row.broadcast_to([TYPES, P])).then_inc(s_in[u], 16)
                    if from_x or ends:
                        if isinstance(i, int) and i == TILES - 1:
                            sp.dma_start(x[0:N - i * P, u, :], dram["x"][i * P:N, :]).then_inc(s_in[u], 16)
                        else:
                            sp.dma_start(x[:, u, :], dram["x"][at, :]).then_inc(s_in[u], 16)
                    if not from_x:
                        sp.dma_start(h_old[:, u, :], dram["h_t"][layer - 1][:, at]).then_inc(s_in[u], 16)

                def stores_of(i, u, k):
                    if ends:
                        return
                    sp.wait_ge(s_hs, i + 1)
                    sp.dma_start(dram["h_t"][layer][:, bass.ds(i * P, P)], h[:, u, :]).then_inc(s_hst[u], 16)
                    sp.wait_ge(s_tk, i + 1)
                    sp.wait_ge(s_tv, i + 1)
                    sp.dma_start(table_out[bass.ds(i * P, P), :, :], table[:, u, :, :]).then_inc(s_tst[u], 16)

                loads_of(0, 0, 0)
                loads_of(1, 1, 0)
                with sp.Fori(1, TILES // 2 - 1) as k:
                    for u in range(2):
                        loads_of(k * 2 + u, u, k)
                        stores_of(k * 2 + (u - 2), u, k - 1)
                k = TILES // 2 - 1
                for i in (TILES - 2, TILES - 1):
                    loads_of(i, i % 2, k)
                    stores_of(i - 2, i % 2, k - 1)
                for i in (TILES - 2, TILES - 1):
                    stores_of(i, i % 2, k)
                if ends:
                    full = TILES - 1
                    sp.wait_ge(s_norm, TILES * 4 + 2 + TILES)
                    sp.dma_start(dram["out"][0:full * P, :].rearrange("(m p) c -> p m c", p=P), q[:, 0:full, :]).then_inc(s_out, 16)
                    sp.dma_start(dram["out"][full * P:N, :], q[0:N - full * P, full, :]).then_inc(s_out, 16)
                    sp.wait_ge(s_out, 32)
                else:
                    for u in range(2):
                        sp.wait_ge(s_hst[u], 16 * (TILES // 2))
                        sp.wait_ge(s_tst[u], 16 * (TILES // 2))

            @block.tensor
            def _(pe):
                ident = const["ident"]
                pe.wait_ge(s_w, mark_loads(from_x, ends))
                pe.wait_ge(s_wv, mark["weights"])

                def turn_inputs(i, u, k):
                    if from_x:
                        pe.wait_ge(s_in[u], (k + 1) * (16 * loads))
                    else:
                        pe.wait_ge(s_g, i + 1)
                    at_least(pe, s_it, i)
                    pe.transpose(in_ps[:, 0:P], (x if from_x else g)[:, u, :], ident[:, :]).then_inc(s_x, 1)

                def linear(i, u):
                    pe.wait_ge(s_it, i + 1)
                    at_least(pe, s_hs, i)
                    if not from_x:
                        pe.matmul(h_ps[:, P:2 * P], stay[:, :], onehot[:, u, :], start=True, stop=True)
                    for t in range(TYPES):
                        pe.matmul(h_ps[:, 0:P], w1[:, t, :], in_typed[:, t, :], start=t == 0, stop=False)
                    pe.matmul(h_ps[:, 0:P], b1[:, :], onehot[:, u, :], start=False, stop=True).then_inc(s_h, 1)

                def project(i, u):
                    if ends:
                        pe.wait_ge(s_hs, i + 1)
                        at_least(pe, s_norm, i * 4)
                        pe.transpose(k_ps[:, 0:P], h[:, u, :], ident[:, :]).then_inc(s_y, 1)
                        return
                    pe.wait_ge(s_ht, i + 1)
                    at_least(pe, s_kv, i)
                    for t in range(TYPES):
                        pe.matmul(qkv_ps[:, 0:P], h_typed[:, t, :], wq[:, t, :], start=t == 0, stop=False)
                    pe.matmul(qkv_ps[:, 0:P], onehot[:, u, :], bq[:, :], start=False, stop=True)
                    for at, w, b in ((P, wk, bk), (2 * P, wv, bv)):
                        for t in range(TYPES):
                            pe.matmul(qkv_ps[:, at:at + P], w[:, t, :], h_typed[:, t, :], start=t == 0, stop=False)
                        last = pe.matmul(qkv_ps[:, at:at + P], b[:, :], onehot[:, u, :], start=False, stop=True)
                    last.then_inc(s_qkv, 1)

                def relate(i, u):
                    if ends:
                        return
                    pe.wait_ge(s_kv, i + 1)
                    at_least(pe, s_tk, i)
                    at_least(pe, s_tv, i)
                    pe.matmul(k_ps[:, :], kv_t[:, 0:P], ak[:, :, :].rearrange("p r c -> p (r c)"), start=True, stop=True)
                    pe.matmul(v_ps[:, :], kv_t[:, P:2 * P], am[:, :, :].rearrange("p r c -> p (r c)"),
                              start=True, stop=True).then_inc(s_tab, 1)

                def turn(new, old):
                    if new:
                        turn_inputs(*new)
                    if old:
                        project(*old[:2])
                    if new:
                        linear(*new[:2])
                    if old:
                        relate(*old[:2])

                over_tiles(pe, turn)


def mark_loads(from_x, ends):
    return 16 * (2 + (0 if from_x else 2) + (0 if ends else 7 + 2 * H))



def edge_phase(nc, dram, const, layer):
    ph = Phase(nc, f"edge{layer}")
    with ph.stack:
        sb, ps = ph.sb, ph.ps
        q, sums, ident, ident16 = (const[n] for n in ("q", "sums", "ident", "ident16"))
        gather_rows, local = sb("gather_rows", [P, 2, SPB], I32), sb("local", [P, 2, SPB], BF16)
        info_ahead, info_behind = sb("info_ahead", [1, 2, SPB], I32), sb("info_behind", [1, 2, 4, SPB], I32)
        links = sb("links", [P, P + 1])
        runs_fwd, runs_bwd = sb("runs_fwd", [1, H, SPB + 1]), sb("runs_bwd", [1, H, SPB + 1])
        kv = sb("kv", [P, 2, SPB, 2 * D])
        onehot = sb("onehot", [P, 2, SPB, P], BF16)
        spread = sb("spread", [P, 2, SPG, P])
        products = sb("products", [P, SPG, P])
        logits = sb("logits", [P, 2, H, SPB])
        scan_a, scan_b = sb("scan_a", [P, P]), sb("scan_b", [P, P])
        ends_fwd, ends_bwd = sb("ends_fwd", [1, H, SPB + 1]), sb("ends_bwd", [1, H, SPB + 1])
        carry_fwd, carry_bwd = sb("carry_fwd", [1, H, SPB + 1]), sb("carry_bwd", [1, H, SPB + 1])
        carry_rows, carry_cols = sb("carry_rows", [1, 2, P]), sb("carry_cols", [P, 2])
        first_max, drop, linked = sb("first_max", [1, H]), sb("drop", [1, H]), sb("linked", [1, 1])
        first_hot, first_cold = sb("first_hot", [1, P]), sb("first_cold", [1, P])
        below, exps = scan_a, scan_b
        keep_share = sb("keep_share", [1, H])
        weights = sb("weights", [P, H, SPB])
        scale, rescaled = sb("scale", [P, H]), sb("rescaled", [P, AW])
        hot32 = sb("hot32", [P, 2, SPG, P])
        weighted = sb("weighted", [P, 2, SPG, AW])
        slot_ps = ph.ps("slot_ps", [P, (SLOTS + 1) * BANK])
        q_ps = ph.ps("q_ps", [P, 2, SPG, P])
        turn_ps = ph.ps("turn_ps", [P, SPG, P], BF16)
        logit_ps = ph.ps("logit_ps", [P, BANK])
        exp_ps = logit_ps[:, P:2 * P]
        row_ps = logit_ps[0:1, P:3 * P]
        col_ps = logit_ps[:, 3 * P:3 * P + 2]
        scale_ps = logit_ps[:, 3 * P + 4:3 * P + 4 + H]

        s_scan, s_pause = ph.sem("s_scan"), ph.sem("s_pause")
        s_plan, s_behind = ([ph.sem(f"{n}{u}") for u in range(2)] for n in ("s_plan", "s_behind"))
        s_kv = [[ph.sem(f"s_kv{u}_{g}") for g in range(GPB)] for u in range(2)]
        (s_set, s_hot, s_hot_t, s_spread, s_q, s_prod, s_logit, s_logit_t, s_ends, s_row, s_chain, s_carry, s_col,
         s_colcopy, s_half, s_below, s_exp, s_exp_t, s_weight, s_scaled, s_hot32, s_weighted, s_step, s_copied) = (
            ph.sem(n) for n in (
                "s_set", "s_hot", "s_hot_t", "s_spread", "s_q", "s_prod", "s_logit", "s_logit_t", "s_ends",
                "s_row", "s_chain", "s_carry", "s_col", "s_colcopy", "s_half", "s_below", "s_exp", "s_exp_t", "s_weight",
                "s_scaled", "s_hot32", "s_weighted", "s_step", "s_copied"))
        SUM_GROUPS = [[], [], [0, 1], [2], [3, 4], [5], [6], [7]]
        CHAIN = 5

        def bodies(engine, body):
            body(0, 0, 0, True, False)
            for b in (1, 2, 3):
                body(b, b % 2, b // 2, True, True)
            with engine.Fori(2, BLOCKS // 2 - 1) as k:
                body(k * 2, 0, k, True, True)
                body(k * 2 + 1, 1, k, True, True)
            for b in (BLOCKS - 2, BLOCKS - 1):
                body(b, b % 2, b // 2, True, True)
            body(BLOCKS, 0, BLOCKS // 2, False, True)

        def pick(engine, ap, high):
            return nc.values_load_multi_w_load_instructions(
                ap, engines=[engine.engine], min_val=0, max_val=high, skip_runtime_bounds_check_because=WHY)[1]

        def pause(engine):
            engine.sem_inc(s_pause, 1)

        with nc.Block() as block:
            @block.sync
            def _(sp):
                def rows_of(b, u):
                    steps = bass.ds(b * SPB, SPB)
                    at_least(sp, s_prod, (b - 1) * GPB)
                    at_least(sp, s_hot, (b - 1) * GPB)
                    sp.dma_start(gather_rows[:, u, :], dram["rows_t"][:, steps]).then_inc(s_plan[u], 16)
                    sp.dma_start(local[:, u, :], dram["local_t"][:, steps]).then_inc(s_plan[u], 16)
                    sp.dma_start(info_ahead[:, u, :], dram["info"][0, steps].unsqueeze(0)).then_inc(s_plan[u], 16)

                def sums_of(b, u):
                    steps = bass.ds(b * SPB, SPB)
                    at_least(sp, s_copied, (b - 1) * SPB)
                    at_least(sp, s_step, (b - 1) * SPB)
                    sp.dma_start(info_behind[:, u, :, :], dram["info"][1:5, steps].unsqueeze(0)).then_inc(s_behind[u], 16)

                def links_of(b):
                    steps = bass.ds(b * SPB, SPB)
                    at_least(sp, s_below, b)
                    for hd in range(H):
                        sp.dma_start(links[hd * SPB:(hd + 1) * SPB, :], dram_ap(
                            dram["link"], b * (SPB * P), [[P, SPB], [1, P + 1]])).then_inc(s_scan, 16)
                    for to, name, at in ((runs_fwd, "run_fwd", 1), (runs_bwd, "run_bwd", 0)):
                        sp.dma_start(to[:, :, at:at + SPB], dram[name][steps].unsqueeze(0).unsqueeze(0).broadcast_to(
                            [1, H, SPB])).then_inc(s_scan, 16)

                rows_of(0, 0)
                rows_of(1, 1)
                sums_of(0, 0)
                sp.wait_ge(s_set, 4)
                links_of(0)
                with sp.Fori(1, BLOCKS // 2) as k:
                    for u in range(2):
                        rows_of(k * 2 + u, u)
                        sums_of(k * 2 + (u - 1), 1 - u)
                        links_of(k * 2 + (u - 1))
                sums_of(BLOCKS - 1, 1)
                links_of(BLOCKS - 1)

            @block.gpsimd
            def _(pool):
                def body(b, u, k, ahead, behind):
                    if not ahead:
                        return
                    for g in range(GPB):
                        if g == 0:
                            pool.wait_ge(s_plan[u], (k + 1) * 48)
                        at_least(pool, s_weighted, (b - 2) * GPB + (g + 1))
                        pause(pool)
                        for j in range(SPG):
                            s = g * SPG + j
                            pool.indirect_dma_start(kv[:, u, s, :], None, dram["table"][layer],
                                                    bass.IndirectOffsetOnAxis(ap=gather_rows[:, u, s:s + 1], axis=0)
                                                    ).then_inc(s_kv[u][g], 16)

                bodies(pool, body)

            @block.vector
            def _(dve):
                for to in (ends_fwd[:, :, 0:1], ends_bwd[:, :, SPB:SPB + 1], runs_fwd[:, :, 0:1],
                           runs_bwd[:, :, SPB:SPB + 1]):
                    dve.memset(to, -BIG).then_inc(s_set, 1)

                def one_hot(b, u, k, g):
                    if g == 0:
                        dve.wait_ge(s_plan[u], (k + 1) * 48)
                    at_least(dve, s_hot32, (b - 2) * GPB + (g + 1))
                    at_least(dve, s_hot_t, (b - 2) * GPB + (g + 1))
                    shape = [P, SPG, P]
                    dve.tensor_tensor(onehot[:, u, g * SPG:(g + 1) * SPG, :], const["column16"][:, :].unsqueeze(1).broadcast_to(shape),
                                      local[:, u, g * SPG:(g + 1) * SPG].unsqueeze(2).broadcast_to(shape),
                                      ALU.is_equal).then_inc(s_hot, 1)

                def multiply(b, u, k, g):
                    dve.wait_ge(s_kv[u][g], (k + 1) * (16 * SPG))
                    dve.wait_ge(s_q, b * GPB + (g + 1))
                    at_least(dve, s_logit, b * GPB + g)
                    dve.tensor_tensor(products[:, :, :], q_ps[:, g % 2, :, :], kv[:, u, g * SPG:(g + 1) * SPG, 0:D],
                                      ALU.mult).then_inc(s_prod, 1)

                def add_up(b, u, k, g):
                    dve.wait_ge(s_prod, b * GPB + (g + 1))
                    if g == 0:
                        at_least(dve, s_logit_t, b - 1)
                    dve.tensor_reduce(logits[:, u, :, g * SPG:(g + 1) * SPG].rearrange("p h s -> p s h"),
                                      products[:, :, :].rearrange("p s (h c) -> p s h c", c=DH),
                                      AX.X, ALU.add).then_inc(s_logit, 1)

                def row_ends(b, w, kw):
                    dve.wait_ge(s_scan, b * (16 * (H + 2)))
                    dve.wait_ge(s_logit_t, b)
                    at_least(dve, s_row, b - 1)
                    dve.tensor_tensor_scan(scan_a[:, :], links[:, 0:P], logit_ps[:, 0:P], -BIG, ALU.add, ALU.max)
                    dve.tensor_tensor_scan(scan_b[:, ::-1], links[:, 1:P + 1][:, ::-1], logit_ps[:, 0:P][:, ::-1], -BIG,
                                           ALU.add, ALU.max).then_inc(s_ends, 1)

                def carries(b, w, kw):
                    base = (b - 1) * CHAIN
                    at = [0]

                    def then(*instructions):
                        at[0] += 1
                        instructions[-1].then_inc(s_chain, 1)
                        dve.wait_ge(s_chain, base + at[0])

                    rows = row_ps.rearrange("o (w h s) -> o w h s", w=2, h=H)
                    flat = lambda ap: ap.rearrange("o h s -> o (h s)")
                    dve.wait_ge(s_set, 4)
                    dve.wait_ge(s_row, b)
                    at_least(dve, s_exp_t, b - 1)
                    then(dve.tensor_copy(ends_fwd[:, :, 1:SPB + 1], rows[:, 0, :, :]),
                         dve.tensor_copy(ends_bwd[:, :, 0:SPB], rows[:, 1, :, :]),
                         dve.tensor_copy(first_hot[:, :], onehot[0:1, w, 0, :]))
                    at_least(dve, s_col, b - 1)
                    at_least(dve, s_exp, b - 1)
                    then(dve.tensor_tensor_scan(flat(carry_fwd[:, :, :]), flat(runs_fwd[:, :, :]), flat(ends_fwd[:, :, :]),
                                                -BIG, ALU.add, ALU.max),
                         dve.tensor_tensor_scan(flat(carry_bwd[:, :, :])[:, ::-1], flat(runs_bwd[:, :, :])[:, ::-1],
                                                flat(ends_bwd[:, :, :])[:, ::-1], -BIG, ALU.add, ALU.max),
                         dve.tensor_scalar(first_cold[:, :], first_hot[:, :], -1.0, 1.0, ALU.mult, ALU.add),
                         dve.tensor_scalar(linked[:, :], links[0:1, 0:1], -1.0, None, ALU.is_ge))
                    then(dve.tensor_copy(carry_rows[:, 0, :].rearrange("o (h s) -> o h s", h=H), carry_fwd[:, :, 0:SPB]),
                         dve.tensor_copy(carry_rows[:, 1, :].rearrange("o (h s) -> o h s", h=H), carry_bwd[:, :, 1:SPB + 1]),
                         dve.tensor_tensor(first_max[:, :], ends_fwd[:, :, 0], carry_bwd[:, :, 0], ALU.max))
                    then(dve.tensor_tensor(drop[:, :], ends_fwd[:, :, 0], first_max[:, :], ALU.subtract))
                    then(dve.tensor_copy(ends_fwd[:, :, 0], carry_fwd[:, :, SPB]))
                    assert at[0] == CHAIN

                def maxima(b, w):
                    dve.wait_ge(s_col, b)
                    dve.tensor_copy(carry_cols[:, :], col_ps).then_inc(s_colcopy, 1)
                    dve.wait_ge(s_colcopy, b)
                    dve.tensor_tensor_scan(scan_a[:, :], links[:, 0:P], logit_ps[:, 0:P], carry_cols[:, 0:1],
                                           ALU.add, ALU.max).then_inc(s_half, 1)
                    dve.wait_ge(s_half, b * 2 - 1)
                    dve.tensor_tensor_scan(scan_b[:, ::-1], links[:, 1:P + 1][:, ::-1], scan_a[:, ::-1], carry_cols[:, 1:2],
                                           ALU.add, ALU.max).then_inc(s_half, 1)
                    dve.wait_ge(s_half, b * 2)
                    dve.tensor_tensor(below[:, :], logit_ps[:, 0:P], scan_b[:, :], ALU.subtract).then_inc(s_below, 1)

                def back_to_edges(b, slot):
                    dve.wait_ge(s_exp_t, b)
                    dve.tensor_copy(weights[:, :, :], exp_ps.rearrange("p (h s) -> p h s", h=H)).then_inc(s_weight, 1)
                    dve.tensor_copy(scale[:, :], scale_ps).then_inc(s_weight, 1)
                    dve.wait_ge(s_weight, b * 2)
                    at_least(dve, s_step, (b - 1) * SPB)
                    dve.tensor_tensor(rescaled[:, :].rearrange("p (h c) -> p h c", c=HW),
                                      slot_ps[:, bass.ds(slot, AW)].rearrange("p (h c) -> p h c", c=HW),
                                      scale[:, :].unsqueeze(2).broadcast_to([P, H, HW]), ALU.mult).then_inc(s_scaled, 1)

                def weigh(b, w, c):
                    done = (b - 1) * GPB + c
                    if c == 0:
                        dve.wait_ge(s_weight, b * 2)
                    at_least(dve, s_step, (done - 1) * SPG)
                    steps = slice(c * SPG, (c + 1) * SPG)
                    to = weighted[:, c % 2, :, :].rearrange("p s (h c) -> p s h c", c=HW)
                    share = weights[:, :, steps].rearrange("p h s -> p s h")
                    dve.tensor_tensor(to[:, :, :, 0:DH], kv[:, w, steps, D:2 * D].rearrange("p s (h c) -> p s h c", c=DH),
                                      share.unsqueeze(3).broadcast_to([P, SPG, H, DH]), ALU.mult)
                    dve.tensor_copy(to[:, :, :, DH], share).then_inc(s_weighted, 1)

                one_hot(0, 0, 0, 0)

                def body(b, u, k, ahead, behind):
                    w, kw = 1 - u, k if u else k - 1
                    if behind and not ahead:
                        dve.wait_ge(s_logit, b * GPB)
                    for g in range(GPB):
                        if ahead:
                            if g < GPB - 1:
                                one_hot(b, u, k, g + 1)
                            elif not (isinstance(b, int) and b == BLOCKS - 1):
                                one_hot(b + 1, 1 - u, k + 1 if u else k, 0)
                        if behind and g == 0:
                            row_ends(b, w, kw)
                        if behind and g == 1:
                            dve.wait_ge(s_behind[w], (kw + 1) * 16)
                            pause(dve)
                            slot, = pick(dve, info_behind[0:1, w, 0, 0:1], (SLOTS - 1) * BANK)
                            maxima(b, w)
                        for c in SUM_GROUPS[g] if behind else ():
                            weigh(b, w, c)
                        if ahead:
                            multiply(b, u, k, g)
                        if ahead:
                            add_up(b, u, k, g)
                        if behind and g == 1:
                            back_to_edges(b, slot)
                        if behind and g == 0:
                            carries(b, w, kw)

                bodies(dve, body)

            @block.scalar
            def _(act):
                def spread_copy(b, u, k, g):
                    act.wait_ge(s_hot_t, b * GPB + (g + 1))
                    at_least(act, s_q, b * GPB + (g - 1))
                    act.activation(spread[:, g % 2, :, :], turn_ps[:, :, :], ACT.Copy).then_inc(s_spread, 1)

                def widen(b, w, c):
                    done = (b - 1) * GPB + c
                    at_least(act, s_step, (done - 1) * SPG)
                    act.activation(hot32[:, c % 2, :, :], onehot[:, w, c * SPG:(c + 1) * SPG, :], ACT.Copy).then_inc(s_hot32, 1)

                def keep_finished(b, w, kw, c):
                    others = pick(act, info_behind[0:1, w, 2, c * SPG:(c + 1) * SPG], (SLOTS - 1) * BANK)
                    places = pick(act, info_behind[0:1, w, 3, c * SPG:(c + 1) * SPG], (TILES - 1) * AW)
                    for j, (other, place) in enumerate(zip(others, places)):
                        s = c * SPG + j
                        at_least(act, s_step, (b - 1) * SPB + s)
                        at_least(act, s_copied, (b - 1) * SPB + s)
                        act.activation(sums[:, :, :].rearrange("p t c -> p (t c)")[:, bass.ds(place, AW)],
                                       slot_ps[:, bass.ds(other, AW)], ACT.Copy).then_inc(s_copied, 1)

                def body(b, u, k, ahead, behind):
                    w, kw = 1 - u, k if u else k - 1
                    for g in range(GPB):
                        if behind and g == 1:
                            act.wait_ge(s_behind[w], (kw + 1) * 16)
                            pause(act)
                            act.wait_ge(s_below, b)
                            at_least(act, s_exp_t, b - 1)
                            act.activation(exps[:, :], below[:, :], ACT.Exp)
                            act.wait_ge(s_chain, b * CHAIN)
                            act.activation(keep_share[:, :], drop[:, :], ACT.Exp, scale=linked[:, :]).then_inc(s_exp, 1)
                        for c in SUM_GROUPS[g] if behind else ():
                            widen(b, w, c)
                        if ahead:
                            if g < GPB - 1:
                                spread_copy(b, u, k, g + 1)
                            elif not (isinstance(b, int) and b == BLOCKS - 1):
                                spread_copy(b + 1, 1 - u, k + 1 if u else k, 0)
                        for c in SUM_GROUPS[g] if behind else ():
                            keep_finished(b, w, kw, c)

                spread_copy(0, 0, 0, 0)
                bodies(act, body)
                act.wait_ge(s_step, STEPS)
                act.wait_ge(s_copied, STEPS)
                act.activation(sums[:, TILES, :], slot_ps[:, ((TILES - 1) % SLOTS) * BANK:((TILES - 1) % SLOTS) * BANK + AW], ACT.Copy)

            @block.tensor
            def _(pe):
                zeros = const["zero16"]
                for slot in range(SLOTS):
                    pe.matmul(slot_ps[:, slot * BANK:slot * BANK + AW], zeros[:, 0:P], zeros[:, :], start=True, stop=True)

                def turn_hot(b, u, k, g):
                    pe.wait_ge(s_hot, b * GPB + (g + 1))
                    at_least(pe, s_spread, b * GPB + g)
                    for j in range(SPG):
                        last = pe.transpose(turn_ps[:, j, :], onehot[:, u, g * SPG + j, :], ident16[:, :])
                    last.then_inc(s_hot_t, 1)

                def spread_q(b, u, k, g):
                    if g == 0:
                        pe.wait_ge(s_plan[u], (k + 1) * 48)
                        pause(pe)
                    columns = pick(pe, info_ahead[0:1, u, g * SPG:(g + 1) * SPG], (TILES - 1) * P)
                    pe.wait_ge(s_spread, b * GPB + (g + 1))
                    at_least(pe, s_prod, b * GPB + (g - 1))
                    for j in range(SPG):
                        last = pe.matmul(q_ps[:, g % 2, j, :], spread[:, g % 2, j, :],
                                         q[:, :, :].rearrange("p t c -> p (t c)")[:, bass.ds(columns[j], P)], start=True, stop=True)
                    last.then_inc(s_q, 1)

                def add_group(b, w, kw, c):
                    slots = pick(pe, info_behind[0:1, w, 0, c * SPG:(c + 1) * SPG], (SLOTS - 1) * BANK)
                    clears = pick(pe, info_behind[0:1, w, 1, c * SPG:(c + 1) * SPG], SLOTS * BANK)
                    pe.wait_ge(s_weighted, (b - 1) * GPB + (c + 1))
                    pe.wait_ge(s_hot32, (b - 1) * GPB + (c + 1))
                    for j in range(SPG):
                        s = c * SPG + j
                        at_least(pe, s_copied, (b - 1) * SPB + (s - 1))
                        pe.matmul(slot_ps[:, bass.ds(clears[j], AW)], zeros[:, 0:P], zeros[:, :], start=True, stop=True)
                        pe.matmul(slot_ps[:, bass.ds(slots[j], AW)], hot32[:, c % 2, j, :], weighted[:, c % 2, j, :],
                                  start=False, stop=True, skip_group_check=True).then_inc(s_step, 1)

                def body(b, u, k, ahead, behind):
                    w, kw = 1 - u, k if u else k - 1
                    for g in range(GPB):
                        if behind and g == 0:
                            pe.wait_ge(s_logit, b * GPB)
                            at_least(pe, s_weight, (b - 1) * 2)
                            pe.transpose(logit_ps[:, 0:P], logits[:, w, :, :].rearrange("p h s -> p (h s)"),
                                         ident[:, :]).then_inc(s_logit_t, 1)
                        if ahead:
                            spread_q(b, u, k, g)
                            if g < GPB - 1:
                                turn_hot(b, u, k, g + 1)
                            elif not (isinstance(b, int) and b == BLOCKS - 1):
                                turn_hot(b + 1, 1 - u, k + 1 if u else k, 0)
                        if not behind:
                            continue
                        if g == 0:
                            pe.wait_ge(s_ends, b)
                            at_least(pe, s_chain, (b - 1) * CHAIN)
                            pe.transpose(row_ps[:, 0:P], scan_a[:, P - 1:P], ident[:, :])
                            pe.transpose(row_ps[:, P:2 * P], scan_b[:, 0:1], ident[:, :]).then_inc(s_row, 1)
                            pe.wait_ge(s_chain, b * CHAIN)
                            at_least(pe, s_colcopy, b - 1)
                            pause(pe)
                            pe.transpose(col_ps[:, 0:1], carry_rows[:, 0, :], ident[0:1, 0:1])
                            pe.transpose(col_ps[:, 1:2], carry_rows[:, 1, :], ident[0:1, 0:1]).then_inc(s_col, 1)
                        if g == 1:
                            pe.wait_ge(s_exp, b)
                            at_least(pe, s_weight, (b - 1) * 2)
                            pe.transpose(exp_ps, exps[:, :], ident[:, :])
                            pe.matmul(scale_ps, first_hot[:, :], keep_share[:, :], start=True, stop=False)
                            pe.matmul(scale_ps, first_cold[:, :], const["ones"][0:1, 0:H], start=False,
                                      stop=True).then_inc(s_exp_t, 1)
                            pe.wait_ge(s_behind[w], (kw + 1) * 16)
                            pause(pe)
                            slot, = pick(pe, info_behind[0:1, w, 0, 0:1], (SLOTS - 1) * BANK)
                            pe.wait_ge(s_scaled, b)
                            at_least(pe, s_copied, (b - 1) * SPB)
                            pe.matmul(slot_ps[:, bass.ds(slot, AW)], ident[:, :], rescaled[:, :], start=True, stop=True)
                        for c in SUM_GROUPS[g]:
                            add_group(b, w, kw, c)

                turn_hot(0, 0, 0, 0)
                bodies(pe, body)



def build_program(nc, args, out):
    def scratch(name, shape, dtype=F32):
        return nc.dram_tensor(f"scratch_{name}", shape, dtype).ap()

    dram = {
        "x": args["x"], "src": args["src"], "dst": args["dst"], "edge_type": args["edge_type_4"],
        "node_type": args["node_type_3"], "out": out,
        "edge_row": scratch("edge_row", [SK * P, P]), "edge_dst": scratch("edge_dst", [SK * P, P]),
        "type_f": scratch("type_f", [NP]), "key": scratch("key", [1 + STEPS * P]),
        "link": scratch("link", [(STEPS + 1) * P]), "run_fwd": scratch("run_fwd", [STEPS]),
        "run_bwd": scratch("run_bwd", [STEPS]), "info": scratch("info", [5, STEPS], I32),
        "rows_t": scratch("rows_t", [P, STEPS], I32), "local_t": scratch("local_t", [P, STEPS], BF16),
        "h_t": scratch("h_t", [2, P, NP]),
        "table": [scratch(f"table{layer}", [RELS * NP, 2 * D]) for layer in range(LAYERS)],
    }
    dram["edge_row_flat"] = dram["edge_row"].rearrange("c e -> (c e)")
    dram["edge_dst_flat"] = dram["edge_dst"].rearrange("c e -> (c e)")
    for short in ("W_in", "b_in", "Wk", "bk", "Wq", "bq", "Wv", "bv", "Wa", "ba", "a_rel", "m_rel", "mu", "skip"):
        dram[short] = args[f"L0_gnn_{short}"]

    keep = Phase(nc, "keep")
    with keep.stack:
        const = {
            "ident": keep.sb("ident", [P, P]), "ident16": keep.sb("ident16", [P, P], BF16),
            "ones": keep.sb("ones", [P, P]), "zero16": keep.sb("zero16", [32, AW], BF16),
            "column16": keep.sb("column16", [P, P], BF16),
            "q": keep.sb("q", [P, TILES, D]), "sums": keep.sb("sums", [P, TILES + 2, AW]),
            "row_i": keep.sb("row_i", [P, 1], I32), "row": keep.sb("row", [P, 1]),
        }
        edge_plan(nc, dram, const)
        for layer in range(LAYERS):
            node_phase(nc, dram, const, layer)
            edge_phase(nc, dram, const, layer)
        node_phase(nc, dram, const, LAYERS)



_INS = ["x", "src", "dst", "edge_type_4", "node_type_3", "L0_gnn_W_in", "L0_gnn_b_in", "L0_gnn_Wk", "L0_gnn_bk",
        "L0_gnn_Wq", "L0_gnn_bq", "L0_gnn_Wv", "L0_gnn_bv", "L0_gnn_Wa", "L0_gnn_ba", "L0_gnn_a_rel", "L0_gnn_m_rel",
        "L0_gnn_mu", "L0_gnn_skip"]


def kernel(**inputs):
    import numpy as _np
    import concourse.bacc as _bacc
    from concourse import mybir as _mybir
    from concourse.bass_utils import run_bass_kernel_spmd as _run

    nc = _bacc.Bacc("TRN2", target_bir_lowering=False, num_devices=1)
    arrays, args = {}, {}
    for name in _INS:
        a = _np.ascontiguousarray(inputs[name])
        arrays[f"in_{name}_dram"] = a
        args[name] = nc.dram_tensor(f"in_{name}_dram", a.shape, _mybir.dt.from_np(a.dtype), kind="ExternalInput").ap()
    out = nc.dram_tensor("out_0_dram", (N, D), _mybir.dt.float32, kind="ExternalOutput").ap()
    build_program(nc, args, out)
    r = _run(nc, [arrays], core_ids=[0])
    return r.results[0]["out_0_dram"]
```

```python
from contextlib import ExitStack

import concourse.bass as bass
from concourse import mybir

F32 = mybir.dt.float32
BF16 = mybir.dt.bfloat16
I32 = mybir.dt.int32
ALU = mybir.AluOpType
ACT = mybir.ActivationFunctionType
AX = mybir.AxisListType

N, E, D = 12500, 200000, 128
H, DH, LAYERS, TYPES, RELS = 4, 32, 2, 3, 4
P = 128
TILES = -(-N // P)
NP = TILES * P
SPB, SPG = 32, 4
GPB = SPB // SPG
BLOCKS = -(-(E // P + TILES) // SPB)
STEPS = BLOCKS * SPB
SK = STEPS // P
EPAD = SK * P * P
EP, EF = 125, E // 125
HW = DH + 1
AW = H * HW
SLOTS = 3
BANK = 512
BIG = 1e38
EPS = 1e-5
FAR = 20000.0
WHY = "computed on the chip from the step number and clamped by construction"


class Phase:

    def __init__(self, nc, tag):
        self.nc, self.tag, self.stack = nc, tag, ExitStack()
        self.semaphores = []
        self.stack.callback(self.clear_semaphores)

    def clear_semaphores(self):
        if self.semaphores:
            self.nc.clear_and_free_semaphores(self.semaphores)
            self.nc.all_engine_barrier()

    def sb(self, name, shape, dtype=F32):
        return self.stack.enter_context(self.nc.sbuf_tensor(f"{self.tag}_{name}", shape, dtype))

    def ps(self, name, shape, dtype=F32):
        return self.stack.enter_context(self.nc.psum_tensor(f"{self.tag}_{name}", shape, dtype))

    def sem(self, name):
        self.semaphores.append(self.nc.alloc_semaphore(f"{self.tag}_{name}"))
        return self.semaphores[-1]


def dram_ap(ap, offset, pattern):
    return bass.AP(tensor=ap.tensor, offset=offset, ap=pattern)


def edge_plan(nc, dram, const):
    ph = Phase(nc, "plan")
    with ph.stack:
        sb, sem = ph.sb, ph.sem
        src_i, et_i, dst_i = (sb(n, [EP, EF], I32) for n in ("src_i", "et_i", "dst_i"))
        row_f, dst_f = sb("row_f", [EP, EF]), sb("dst_f", [EP, EF])
        TW = 112
        TP = (EPAD - E) // TW
        tail_row, tail_dst = sb("tail_row", [TP, TW]), sb("tail_dst", [TP, TW])
        type_i, type_f = sb("type_i", [100, N // 100], I32), sb("type_f", [100, N // 100])
        zeros = sb("zeros", [1, P])
        last = sb("last", [P, SK])
        tile_i, tile_id = sb("tile_i", [P, TILES], I32), sb("tile_id", [P, TILES])
        tile_start = sb("tile_start", [P, TILES])
        column_i, parity_i, parity = sb("column_i", [P, P], I32), sb("parity_i", [P, P], I32), sb("parity", [P, P])
        spare, place = sb("spare", [P, 1]), sb("place", [P, SK])
        step_i, step_f = sb("step_i", [P, SK], I32), sb("step_f", [P, SK])
        compare = sb("compare", [P, SK, TILES])
        chunks_before = sb("chunks_before", [P, TILES])
        first_step = sb("first_step", [P, TILES])
        tile_of, tile_base, is_first = sb("tile_of", [P, SK]), sb("tile_base", [P, SK]), sb("is_first", [P, SK])
        chunk_i = sb("chunk_i", [P, SK], I32)
        tile_slot_i, tile_slot = sb("tile_slot_i", [P, -(-TILES // SLOTS) * SLOTS], I32), sb("tile_slot", [P, -(-TILES // SLOTS) * SLOTS])
        slot_of, slot_wrap, info = sb("slot_of", [P, SK]), sb("slot_wrap", [P, SK]), sb("info", [P, 5, SK], I32)
        rows, dsts = sb("rows", [P, SK, P]), sb("dsts", [P, SK, P])
        local, inside, key = sb("local", [P, SK, P]), sb("inside", [P, SK, P]), sb("key", [P, SK, P])
        before, link = sb("before", [P, SK, P]), sb("link", [P, SK, P])
        whole, link_next = sb("whole", [P, SK]), sb("link_next", [P, SK])
        run_fwd, run_bwd = sb("run_fwd", [P, SK]), sb("run_bwd", [P, SK])
        big_row = sb("big_row", [1, P])
        rows_t, local_t = sb("rows_t", [P, STEPS], I32), sb("local_t", [P, STEPS], BF16)
        count_ps = ph.ps("count_ps", [P, TILES])
        turn_ps = ph.ps("turn_ps", [P, 2, BANK])
        s_load, s_type, s_flat, s_last = sem("s_load"), sem("s_type"), sem("s_flat"), sem("s_last")
        s_set, s_io, s_v, s_cnt, s_gather = sem("s_set"), sem("s_io"), sem("s_v"), sem("s_cnt"), sem("s_gather")
        s_key, s_before, s_link, s_next, s_t, s_tc, s_out = (
            sem(n) for n in ("s_key", "s_before", "s_link", "s_next", "s_t", "s_tc", "s_out"))
        mark = {}

        def by_step(ap):
            return ap.rearrange("(k p) -> p k", p=P)

        with nc.Block() as block:
            @block.vector
            def _(dve):
                count = [0]

                def then(instruction):
                    count[0] += 1
                    instruction.then_inc(s_v, 1)
                    dve.wait_ge(s_v, count[0])

                dve.wait_ge(s_load, 48)
                dve.wait_ge(s_type, 16)
                then(dve.scalar_tensor_tensor(out=row_f[:, :], in0=et_i[:, :], scalar=float(NP), in1=src_i[:, :], op0=ALU.mult, op1=ALU.add))
                then(dve.tensor_copy(dst_f[:, :], dst_i[:, :]))
                then(dve.tensor_copy(type_f[:, :], type_i[:, :]))
                mark["flat"] = count[0]
                dve.wait_ge(s_io, 6)
                then(dve.tensor_copy(tile_id[:, :], tile_i[:, :]))
                then(dve.tensor_copy(step_f[:, :], step_i[:, :]))
                then(dve.tensor_copy(tile_slot[:, :], tile_slot_i[:, :]))
                then(dve.tensor_copy(const["column16"][:, :], column_i[:, :]))
                then(dve.tensor_copy(const["row"][:, :], const["row_i"][:, :]))
                then(dve.tensor_scalar(tile_start[:, :], tile_id[:, :], float(P), None, ALU.mult))
                dve.wait_ge(s_set, 8)
                then(dve.tensor_copy(const["ident16"][:, :], const["ident"][:, :]))
                dve.wait_ge(s_last, 16)
                wide = [P, SK, TILES]
                then(dve.tensor_tensor(compare[:, :, :], last[:, :].unsqueeze(2).broadcast_to(wide),
                                               tile_start[:, :].unsqueeze(1).broadcast_to(wide), ALU.is_lt))
                then(dve.tensor_reduce(chunks_before[:, :], compare[:, :, :].rearrange("p k t -> p t k"), AX.X, ALU.add))
                mark["count"] = count[0]
                dve.wait_ge(s_cnt, 1)
                then(dve.tensor_tensor(first_step[:, :], count_ps[:, :], tile_id[:, :], ALU.add))
                by_tile = lambda: (first_step[:, :].unsqueeze(1).broadcast_to(wide), step_f[:, :].unsqueeze(2).broadcast_to(wide))
                then(dve.tensor_tensor(compare[:, :, :], *by_tile(), ALU.is_le))
                then(dve.tensor_reduce(tile_of[:, :], compare[:, :, :], AX.X, ALU.add))
                then(dve.tensor_tensor(compare[:, :, :], *by_tile(), ALU.is_equal))
                then(dve.tensor_reduce(is_first[:, :], compare[:, :, :], AX.X, ALU.add))
                then(dve.tensor_scalar(tile_of[:, :], tile_of[:, :], -1.0, None, ALU.add))
                then(dve.tensor_tensor(chunk_i[:, :], step_f[:, :], tile_of[:, :], ALU.subtract))
                mark["chunk"] = count[0]
                then(dve.tensor_scalar(tile_base[:, :], tile_of[:, :], float(P), None, ALU.mult))
                then(dve.tensor_tensor(compare[:, :, :], tile_of[:, :].unsqueeze(2).broadcast_to(wide),
                                       tile_id[:, :].unsqueeze(1).broadcast_to(wide), ALU.is_equal))
                then(dve.tensor_tensor(compare[:, :, :], compare[:, :, :], tile_slot[:, 0:TILES].unsqueeze(1).broadcast_to(wide), ALU.mult))
                then(dve.tensor_reduce(slot_of[:, :], compare[:, :, :], AX.X, ALU.add))
                then(dve.tensor_copy(info[:, 0, :], tile_base[:, :]))
                then(dve.tensor_scalar(info[:, 1, :], slot_of[:, :], float(BANK), None, ALU.mult))
                then(dve.scalar_tensor_tensor(out=is_first[:, :], in0=slot_of[:, :], scalar=-float(SLOTS), in1=is_first[:, :],
                                              op0=ALU.add, op1=ALU.mult))
                then(dve.tensor_scalar(info[:, 2, :], is_first[:, :], float(BANK), float(SLOTS * BANK), ALU.mult, ALU.add))
                then(dve.tensor_scalar(slot_wrap[:, :], slot_of[:, :], 1.0, -float(SLOTS), ALU.is_ge, ALU.mult))
                then(dve.tensor_tensor(slot_wrap[:, :], slot_wrap[:, :], slot_of[:, :], ALU.add))
                then(dve.tensor_scalar(info[:, 3, :], slot_wrap[:, :], float(BANK), float((SLOTS - 1) * BANK), ALU.mult, ALU.add))
                then(dve.tensor_copy(parity[:, :], parity_i[:, :]))
                then(dve.tensor_tensor(parity[:, :], parity[:, :], const["ident"][:, :], ALU.mult))
                then(dve.tensor_reduce(spare[:, :], parity[:, :], AX.X, ALU.add))
                then(dve.tensor_scalar(spare[:, :], spare[:, :], float((TILES + 1) * AW), None, ALU.mult))
                then(dve.tensor_scalar(place[:, :], tile_of[:, :], float(AW), spare[:, :], ALU.mult, ALU.subtract))
                then(dve.scalar_tensor_tensor(out=place[:, :], in0=is_first[:, :], scalar=0.0, in1=place[:, :],
                                              op0=ALU.is_lt, op1=ALU.mult))
                then(dve.tensor_scalar(info[:, 4, :], place[:, :], spare[:, :], None, ALU.add))
                dve.wait_ge(s_gather, 16 * 2 * SK)
                full = [P, SK, P]
                then(dve.tensor_tensor(local[:, :, :], dsts[:, :, :], tile_base[:, :].unsqueeze(2).broadcast_to(full), ALU.subtract))
                then(dve.tensor_scalar(local[:, :, :], local[:, :, :], -1.0, float(P), ALU.max, ALU.min))
                then(dve.tensor_scalar(inside[:, :, :], local[:, :, :], 0.0, float(P - 1), ALU.max, ALU.min))
                then(dve.tensor_tensor(inside[:, :, :], inside[:, :, :], local[:, :, :], ALU.is_equal))
                then(dve.scalar_tensor_tensor(out=key[:, :, :], in0=dsts[:, :, :], scalar=1.0, in1=inside[:, :, :], op0=ALU.add, op1=ALU.mult))
                mark["key"] = count[0]
                dve.wait_ge(s_before, 16)
                then(dve.tensor_tensor(link[:, :, :], key[:, :, :], before[:, :, :], ALU.is_equal))
                then(dve.scalar_tensor_tensor(out=link[:, :, :], in0=key[:, :, :], scalar=0.0, in1=link[:, :, :], op0=ALU.is_gt, op1=ALU.mult))
                then(dve.tensor_scalar(link[:, :, :], link[:, :, :], -1.0, BIG, ALU.add, ALU.mult))
                mark["link"] = count[0]
                then(dve.tensor_reduce(whole[:, :], link[:, :, 1:P], AX.X, ALU.min))
                then(dve.tensor_tensor(run_fwd[:, :], whole[:, :], link[:, :, 0], ALU.min))
                dve.wait_ge(s_next, 16)
                then(dve.tensor_tensor(run_bwd[:, :], whole[:, :], link_next[:, :], ALU.min))
                mark["runs"] = count[0]
                for k in range(SK):
                    for m, out in ((0, rows_t), (1, local_t)):
                        dve.wait_ge(s_t, 2 * k + m + 1)
                        dve.tensor_copy(out[:, k * P:(k + 1) * P], turn_ps[:, m, 0:P]).then_inc(s_tc, 1)

            @block.gpsimd
            def _(pool):
                pool.memset(const["ident"][:, :], 0.0).then_inc(s_set, 1)
                pool.memset(const["ones"][:, :], 1.0).then_inc(s_set, 1)
                pool.memset(const["zero16"][:, :], 0.0).then_inc(s_set, 1)
                pool.memset(zeros[:, :], 0.0).then_inc(s_set, 1)
                pool.memset(big_row[:, :], -BIG).then_inc(s_set, 1)
                pool.memset(tail_row[:, :], 0.0).then_inc(s_set, 1)
                pool.memset(tail_dst[:, :], FAR).then_inc(s_set, 1)
                pool.iota(tile_i[:, :], [[1, TILES]], base=0, channel_multiplier=0).then_inc(s_io, 1)
                pool.iota(tile_slot_i[:, :], [[0, -(-TILES // SLOTS)], [1, SLOTS]], base=0, channel_multiplier=0).then_inc(s_io, 1)
                pool.iota(parity_i[:, :], [[0, P // 2], [1, 2]], base=0, channel_multiplier=0).then_inc(s_io, 1)
                pool.iota(step_i[:, :], [[P, SK]], base=0, channel_multiplier=1).then_inc(s_io, 1)
                pool.iota(column_i[:, :], [[1, P]], base=0, channel_multiplier=0).then_inc(s_io, 1)
                pool.iota(const["row_i"][:, :], [[1, 1]], base=0, channel_multiplier=1).then_inc(s_io, 1)
                pool.memset(const["sums"][:, TILES + 1, :], 0.0)
                pool.wait_ge(s_set, 7)
                pool.affine_select(out=const["ident"][:, :], in_=const["ident"][:, :], compare_op=ALU.not_equal,
                                   fill=1.0, base=0, pattern=[[-1, P]], channel_multiplier=1).then_inc(s_set, 1)
                pool.wait_ge(s_flat, 64)
                pool.wait_ge(s_v, mark["chunk"])
                for k in range(SK):
                    for to, table in ((rows, dram["edge_row"]), (dsts, dram["edge_dst"])):
                        pool.indirect_dma_start(
                            to[:, k, :], None, table,
                            bass.IndirectOffsetOnAxis(ap=chunk_i[:, k:k + 1], axis=0)).then_inc(s_gather, 16)

            @block.sync
            def _(sp):
                for to, name in ((src_i, "src"), (et_i, "edge_type"), (dst_i, "dst")):
                    sp.dma_start(to[:, :], dram[name].rearrange("(p n) -> p n", p=EP)).then_inc(s_load, 16)
                sp.dma_start(type_i[:, :], dram["node_type"].rearrange("(p n) -> p n", p=100)).then_inc(s_type, 16)
                sp.wait_ge(s_set, 8)
                sp.dma_start(dram["edge_row_flat"][E:EPAD].rearrange("(p n) -> p n", p=TP), tail_row[:, :]).then_inc(s_flat, 16)
                sp.dma_start(dram["edge_dst_flat"][E:EPAD].rearrange("(p n) -> p n", p=TP), tail_dst[:, :]).then_inc(s_flat, 16)
                sp.dma_start(dram["type_f"][N:NP].unsqueeze(0), zeros[:, 0:NP - N]).then_inc(s_out, 16)
                sp.dma_start(dram["key"][0:1].unsqueeze(0), zeros[:, 0:1]).then_inc(s_key, 16)
                sp.dma_start(dram["link"][STEPS * P:(STEPS + 1) * P].unsqueeze(0), big_row[:, :]).then_inc(s_link, 16)
                sp.wait_ge(s_v, mark["flat"])
                sp.dma_start(dram["edge_row_flat"][0:E].rearrange("(p n) -> p n", p=EP), row_f[:, :]).then_inc(s_flat, 16)
                sp.dma_start(dram["edge_dst_flat"][0:E].rearrange("(p n) -> p n", p=EP), dst_f[:, :]).then_inc(s_flat, 16)
                sp.dma_start(dram["type_f"][0:N].rearrange("(p n) -> p n", p=100), type_f[:, :]).then_inc(s_out, 16)
                sp.wait_ge(s_flat, 64)
                sp.dma_start(last[:, :], by_step(dram["edge_dst"][:, P - 1]), allow_slow_non_contiguous=True).then_inc(s_last, 16)
                sp.wait_ge(s_v, mark["key"])
                sp.dma_start(dram["key"][1:1 + STEPS * P].rearrange("(k p e) -> p k e", p=P, e=P), key[:, :, :]).then_inc(s_key, 16)
                sp.wait_ge(s_key, 32)
                sp.dma_start(before[:, :, :], dram["key"][0:STEPS * P].rearrange("(k p e) -> p k e", p=P, e=P)).then_inc(s_before, 16)
                sp.wait_ge(s_v, mark["link"])
                sp.dma_start(dram["link"][0:STEPS * P].rearrange("(k p e) -> p k e", p=P, e=P), link[:, :, :]).then_inc(s_link, 16)
                sp.wait_ge(s_link, 32)
                sp.dma_start(link_next[:, :], dram_ap(dram["link"], P, [[P, P], [P * P, SK]]),
                             allow_slow_non_contiguous=True).then_inc(s_next, 16)
                sp.wait_ge(s_v, mark["runs"])
                sp.dma_start(by_step(dram["run_fwd"]), run_fwd[:, :], allow_slow_non_contiguous=True).then_inc(s_out, 16)
                sp.dma_start(by_step(dram["run_bwd"]), run_bwd[:, :], allow_slow_non_contiguous=True).then_inc(s_out, 16)
                for c in range(5):
                    sp.dma_start(by_step(dram["info"][c, :]), info[:, c, :], allow_slow_non_contiguous=True).then_inc(s_out, 16)
                sp.wait_ge(s_tc, 2 * SK)
                sp.dma_start(dram["rows_t"], rows_t[:, :]).then_inc(s_out, 16)
                sp.dma_start(dram["local_t"], local_t[:, :]).then_inc(s_out, 16)
                sp.wait_ge(s_out, 16 * 11)

            @block.tensor
            def _(pe):
                pe.wait_ge(s_set, 8)
                pe.wait_ge(s_v, mark["count"])
                pe.matmul(count_ps[:, :], const["ones"][:, :], chunks_before[:, :], start=True, stop=True).then_inc(s_cnt, 1)
                pe.wait_ge(s_gather, 16 * 2 * SK)
                pe.wait_ge(s_v, mark["key"])
                for k in range(SK):
                    for m, what in ((0, rows), (1, local)):
                        if k:
                            pe.wait_ge(s_tc, 2 * (k - 1) + m + 1)
                        pe.transpose(turn_ps[:, m, 0:P], what[:, k, :], const["ident"][:, :]).then_inc(s_t, 1)



def at_least(engine, semaphore, value):
    if not isinstance(value, int) or value > 0:
        engine.wait_ge(semaphore, value)


def split_in_three(dve, then, rest, thirds):
    then(dve.tensor_copy(thirds, rest))
    then(dve.tensor_tensor(rest, rest, thirds, ALU.subtract))
    then(dve.tensor_copy(thirds[32:64], rest[32:64]))
    then(dve.tensor_copy(thirds[64:96], rest[64:96]))
    then(dve.tensor_tensor(rest[64:96], rest[64:96], thirds[64:96], ALU.subtract))
    then(dve.tensor_copy(thirds[64:96], rest[64:96]))


def node_phase(nc, dram, const, layer):
    from_x = layer == 0
    ph = Phase(nc, f"node{layer}")
    with ph.stack:
        sb, ps, sem = ph.sb, ph.ps, ph.sem
        q, sums = const["q"], const["sums"]
        w1 = sb("w1", [P, TYPES, P])
        B1, BQ, BK, BV, STAY = range(5)
        rows, rows16 = sb("rows", [P, 5, P]), sb("rows16", [P, 5, P], BF16)
        row_type, above = sb("row_type", [P, 1]), sb("above", [P, 1])
        if not from_x:
            skip_all, skip_col = sb("skip_all", [P, TYPES]), sb("skip_col", [P, 1])
            weight, recip = sb("weight", [P, H]), sb("recip", [P, 2, H])
            mean_v, g = sb("mean_v", [P, 2, P]), sb("g", [P, 2, P])
            h_old, stayed = sb("h_old", [P, 2, P]), sb("stayed", [P, P])
        wq, wk, wv = (sb(n, [P, TYPES, P]) for n in ("wq", "wk", "wv"))
        ak, am = sb("ak", [P, RELS, P]), sb("am", [P, RELS, P])
        mu = sb("mu", [P, RELS * H])
        h_typed, kv_t = sb("h_typed", [P, TYPES, P]), sb("kv_t", [P, 2 * P])
        table = sb("table", [P, 2, RELS, 2 * P])
        x = sb("x", [P, 2, P])
        types, onehot = sb("types", [P, 2, P]), sb("onehot", [P, 2, P], BF16)
        in_typed, h = sb("in_typed", [P, TYPES, P]), sb("h", [P, 2, P])
        in_ps, h_ps, qkv_ps = ps("in_ps", [P, BANK]), ps("h_ps", [P, BANK]), ps("qkv_ps", [P, BANK])
        k_ps, v_ps = ps("k_ps", [P, BANK]), ps("v_ps", [P, BANK])
        s_w, s_wv, s_ws, s_chain = (sem(n) for n in ("s_w", "s_wv", "s_ws", "s_chain"))
        s_in, s_hst, s_tst = ([sem(f"{n}{u}") for u in range(2)] for n in ("s_in", "s_hst", "s_tst"))
        s_mean, s_g, s_x, s_it, s_h, s_stay, s_hs, s_ht = (
            sem(n) for n in ("s_mean", "s_g", "s_x", "s_it", "s_h", "s_stay", "s_hs", "s_ht"))
        s_qkv, s_kv, s_tab, s_tk, s_tv = (sem(n) for n in ("s_qkv", "s_kv", "s_tab", "s_tk", "s_tv"))
        mark = {}
        loads = 2
        table_out = dram["table"][layer].rearrange("(r n) c -> n r c", r=RELS)

        def over_tiles(engine, turn):
            turn((0, 0, 0), None)
            for i in (1, 2, 3):
                turn((i, i % 2, i // 2), (i - 1, (i - 1) % 2, (i - 1) // 2))
            with engine.Fori(2, TILES // 2) as k:
                turn((k * 2, 0, k), (k * 2 - 1, 1, k - 1))
                turn((k * 2 + 1, 1, k), (k * 2, 0, k))
            turn(None, (TILES - 1, 1, TILES // 2 - 1))

        def is_tile(i, number):
            return isinstance(i, int) and i == number

        with nc.Block() as block:
            @block.vector
            def _(dve):
                count = [0]

                def then(instruction):
                    count[0] += 1
                    instruction.then_inc(s_wv, 1)
                    dve.wait_ge(s_wv, count[0])

                then(dve.memset(ak[:, :, :], 0.0))
                then(dve.memset(am[:, :, :], 0.0))
                then(dve.memset(rows[:, :, :], 0.0))
                if not from_x:
                    then(dve.memset(skip_col[:, :], 0.0))
                mark["cleared"] = count[0]
                then(dve.tensor_scalar(row_type[:, :], const["row"][:, :], 32.0, -32.0, ALU.is_ge, ALU.mult))
                then(dve.tensor_tensor(row_type[:, :], row_type[:, :], const["row"][:, :], ALU.add))
                then(dve.tensor_scalar(above[:, :], const["row"][:, :], 64.0, -32.0, ALU.is_ge, ALU.mult))
                then(dve.tensor_tensor(row_type[:, :], row_type[:, :], above[:, :], ALU.add))
                dve.wait_ge(s_w, mark_loads(from_x))
                blocks = [P, RELS * H, DH]
                flat = ak[:, :, :].rearrange("p r (h e) -> p (r h) e", e=DH)
                then(dve.scalar_tensor_tensor(out=flat, in0=flat, scalar=float(DH) ** -0.5, op0=ALU.mult,
                                              in1=mu[:, :].unsqueeze(2).broadcast_to(blocks), op1=ALU.mult))
                if not from_x:
                    dve.wait_ge(s_ws, 1)
                    for t in range(TYPES):
                        then(dve.tensor_scalar(w1[:, t, :], w1[:, t, :], skip_all[:, t:t + 1], None, ALU.mult))
                    then(dve.tensor_scalar(rows[:, B1, :], rows[:, B1, :], skip_col[:, :], None, ALU.mult))
                    then(dve.tensor_scalar(rows[:, STAY, :], const["ones"][:, :], skip_col[:, :], None, ALU.mult))
                    then(dve.tensor_scalar(rows[:, STAY, :], rows[:, STAY, :], -1.0, 1.0, ALU.mult, ALU.add))
                split_in_three(dve, then, rows[:, :, :], rows16[:, :, :])
                mark["weights"] = count[0]
                def mean(i, u):
                    at_least(dve, s_g, i - 1)
                    one = sums[:, bass.ds(i + 1, 1), :].rearrange("p o (h c) -> p (o h) c", c=HW)
                    dve.tensor_scalar(weight[:, :], one[:, :, DH], 1e-16, None, ALU.add).then_inc(s_chain, 1)
                    dve.wait_ge(s_chain, i * 2 + 1)
                    dve.reciprocal(recip[:, u, :], weight[:, :]).then_inc(s_chain, 1)
                    dve.wait_ge(s_chain, i * 2 + 2)
                    dve.tensor_tensor(mean_v[:, u, :].rearrange("p (h c) -> p h c", c=DH), one[:, :, 0:DH],
                                      recip[:, u, :].unsqueeze(2).broadcast_to([P, H, DH]), ALU.mult).then_inc(s_mean, 1)

                def first_half(i, u, k):
                    if is_tile(i, 0) and not from_x:
                        mean(0, 0)
                    dve.wait_ge(s_in[u], (k + 1) * (16 * loads))
                    dve.wait_ge(s_x, i + 1)
                    at_least(dve, s_h, i)
                    at_least(dve, s_qkv, i - 1)
                    for t in range(TYPES):
                        dve.scalar_tensor_tensor(out=in_typed[:, t, :], in0=types[:, u, :], scalar=float(t),
                                                 in1=in_ps[:, 0:P], op0=ALU.is_equal, op1=ALU.mult)
                    dve.tensor_scalar(onehot[:, u, :], types[:, u, :], row_type[:, :], None,
                                      ALU.is_equal).then_inc(s_it, 1)
                    if not from_x:
                        mean(i + 1, 1 - u)
                        dve.wait_ge(s_h, i + 1)
                        at_least(dve, s_hs, i)
                        dve.tensor_tensor(stayed[:, :], h_ps[:, P:2 * P], h_old[:, u, :], ALU.mult).then_inc(s_stay, 1)
                        dve.wait_ge(s_stay, i + 1)
                        at_least(dve, s_ht, i - 1)
                        at_least(dve, s_hst[u], k * 16)
                        dve.tensor_tensor(h[:, u, :], stayed[:, :], h_ps[:, 0:P], ALU.add).then_inc(s_hs, 1)
                    dve.wait_ge(s_hs, i + 1)
                    at_least(dve, s_qkv, i)
                    for t in range(TYPES):
                        last = dve.scalar_tensor_tensor(out=h_typed[:, t, :], in0=types[:, u, :], scalar=float(t),
                                                        in1=h[:, u, :], op0=ALU.is_equal, op1=ALU.mult)
                    last.then_inc(s_ht, 1)

                def second_half(i, u, k):
                    dve.wait_ge(s_tab, i + 1)
                    at_least(dve, s_tst[u], k * 16)
                    dve.tensor_copy(table[:, u, :, 0:P], k_ps[:, :].rearrange("p (r c) -> p r c", c=P)).then_inc(s_tk, 1)

                def turn(new, old):
                    if new:
                        first_half(*new)
                    if old:
                        second_half(*old)

                over_tiles(dve, turn)

            @block.scalar
            def _(act):
                if not from_x:
                    act.wait_ge(s_w, mark_loads(from_x))
                    act.activation(skip_all[:, :], skip_all[:, :], ACT.Sigmoid)
                    act.activation(skip_col[:, :], skip_col[:, :], ACT.Sigmoid).then_inc(s_ws, 1)

                def gelu(i, u):
                    act.wait_ge(s_mean, i + 1)
                    at_least(act, s_x, i - 1)
                    act.activation(g[:, u, :], mean_v[:, u, :], ACT.Gelu_apprx_tanh).then_inc(s_g, 1)

                def turn(new, old):
                    if old:
                        i, u, k = old
                        act.wait_ge(s_qkv, i + 1)
                        act.activation(q[:, bass.ds(i, 1), :].rearrange("p o c -> p (o c)"), qkv_ps[:, 0:P], ACT.Copy)
                        at_least(act, s_tab, i)
                        act.activation(kv_t[:, :], qkv_ps[:, P:3 * P], ACT.Copy).then_inc(s_kv, 1)
                    if new and from_x:
                        i, u, k = new
                        act.wait_ge(s_h, i + 1)
                        at_least(act, s_ht, i - 1)
                        at_least(act, s_hst[u], k * 16)
                        act.activation(h[:, u, :], h_ps[:, 0:P], ACT.Copy).then_inc(s_hs, 1)
                    if new and not from_x:
                        i, u, k = new
                        if is_tile(i, 0):
                            gelu(0, 0)
                        gelu(i + 1, 1 - u)
                    if old:
                        i, u, k = old
                        act.wait_ge(s_tab, i + 1)
                        at_least(act, s_tst[u], k * 16)
                        act.activation(table[:, u, :, P:2 * P], v_ps[:, :].rearrange("p (r c) -> p r c", c=P),
                                       ACT.Copy).then_inc(s_tv, 1)

                over_tiles(act, turn)

            @block.sync
            def _(sp):
                w_name, b_name = ("W_in", "b_in") if from_x else ("Wa", "ba")
                pick = (lambda name: dram[name]) if from_x else (lambda name: dram[name][layer - 1])
                to_in = lambda ap: ap.rearrange("t i o -> i t o")
                sp.dma_start(w1[:, :, :], to_in(pick(w_name))).then_inc(s_w, 16)
                for to, name in ((wq, "Wq"), (wk, "Wk"), (wv, "Wv")):
                    sp.dma_start(to[:, :, :], to_in(dram[name][layer])).then_inc(s_w, 16)
                sp.dma_start(mu[:, :], dram["mu"][layer].rearrange("r h -> (r h)").unsqueeze(0).broadcast_to(
                    [P, RELS * H])).then_inc(s_w, 16)
                sp.wait_ge(s_wv, mark["cleared"])
                for at in (0, 32, 64):
                    part = slice(at, at + TYPES)
                    sp.dma_start(rows[part, B1, :], pick(b_name)).then_inc(s_w, 16)
                    for which, name in ((BQ, "bq"), (BK, "bk"), (BV, "bv")):
                        sp.dma_start(rows[part, which, :], dram[name][layer]).then_inc(s_w, 16)
                    if not from_x:
                        sp.dma_start(skip_col[part, :], dram["skip"][layer - 1].unsqueeze(1),
                                     allow_slow_non_contiguous=True).then_inc(s_w, 16)
                if not from_x:
                    sp.dma_start(skip_all[:, :], dram["skip"][layer - 1].unsqueeze(0).broadcast_to(
                        [P, TYPES])).then_inc(s_w, 16)
                for to, name in ((ak, "a_rel"), (am, "m_rel")):
                    for hd in range(H):
                        part = slice(hd * DH, (hd + 1) * DH)
                        sp.dma_start(to[part, :, part], dram[name][layer][:, hd, :, :].rearrange(
                            "r d e -> d r e")).then_inc(s_w, 16)

                def loads_of(i, u, k):
                    at_least(sp, s_ht, i - 1)
                    at = bass.ds(i * P, P)
                    row = dram["type_f"][at].unsqueeze(0)
                    sp.dma_start(types[:, u, :], row.broadcast_to([P, P])).then_inc(s_in[u], 16)
                    if from_x:
                        if isinstance(i, int) and i == TILES - 1:
                            sp.dma_start(x[0:N - i * P, u, :], dram["x"][i * P:N, :]).then_inc(s_in[u], 16)
                        else:
                            sp.dma_start(x[:, u, :], dram["x"][at, :]).then_inc(s_in[u], 16)
                    else:
                        sp.dma_start(h_old[:, u, :], dram["h_t"][layer - 1][:, at]).then_inc(s_in[u], 16)

                def stores_of(i, u, k):
                    sp.wait_ge(s_hs, i + 1)
                    sp.dma_start(dram["h_t"][layer][:, bass.ds(i * P, P)], h[:, u, :]).then_inc(s_hst[u], 16)
                    sp.wait_ge(s_tk, i + 1)
                    sp.wait_ge(s_tv, i + 1)
                    sp.dma_start(table_out[bass.ds(i * P, P), :, :], table[:, u, :, :]).then_inc(s_tst[u], 16)

                loads_of(0, 0, 0)
                loads_of(1, 1, 0)
                with sp.Fori(1, TILES // 2 - 1) as k:
                    for u in range(2):
                        loads_of(k * 2 + u, u, k)
                        stores_of(k * 2 + (u - 2), u, k - 1)
                k = TILES // 2 - 1
                for i in (TILES - 2, TILES - 1):
                    loads_of(i, i % 2, k)
                    stores_of(i - 2, i % 2, k - 1)
                for i in (TILES - 2, TILES - 1):
                    stores_of(i, i % 2, k)
                for u in range(2):
                    sp.wait_ge(s_hst[u], 16 * (TILES // 2))
                    sp.wait_ge(s_tst[u], 16 * (TILES // 2))

            @block.tensor
            def _(pe):
                ident = const["ident"]
                pe.wait_ge(s_w, mark_loads(from_x))
                pe.wait_ge(s_wv, mark["weights"])

                def turn_inputs(i, u, k):
                    if from_x:
                        pe.wait_ge(s_in[u], (k + 1) * (16 * loads))
                    else:
                        pe.wait_ge(s_g, i + 1)
                    at_least(pe, s_it, i)
                    pe.transpose(in_ps[:, 0:P], (x if from_x else g)[:, u, :], ident[:, :]).then_inc(s_x, 1)

                def linear(i, u):
                    pe.wait_ge(s_it, i + 1)
                    at_least(pe, s_hs, i)
                    if not from_x:
                        pe.matmul(h_ps[:, P:2 * P], rows16[:, STAY, :], onehot[:, u, :], start=True, stop=True)
                    for t in range(TYPES):
                        pe.matmul(h_ps[:, 0:P], w1[:, t, :], in_typed[:, t, :], start=t == 0, stop=False)
                    pe.matmul(h_ps[:, 0:P], rows16[:, B1, :], onehot[:, u, :], start=False, stop=True).then_inc(s_h, 1)

                def project(i, u):
                    pe.wait_ge(s_ht, i + 1)
                    at_least(pe, s_kv, i)
                    for t in range(TYPES):
                        pe.matmul(qkv_ps[:, 0:P], h_typed[:, t, :], wq[:, t, :], start=t == 0, stop=False)
                    pe.matmul(qkv_ps[:, 0:P], onehot[:, u, :], rows16[:, BQ, :], start=False, stop=True)
                    for at, w, b in ((P, wk, BK), (2 * P, wv, BV)):
                        for t in range(TYPES):
                            pe.matmul(qkv_ps[:, at:at + P], w[:, t, :], h_typed[:, t, :], start=t == 0, stop=False)
                        last = pe.matmul(qkv_ps[:, at:at + P], rows16[:, b, :], onehot[:, u, :], start=False, stop=True)
                    last.then_inc(s_qkv, 1)

                def relate(i, u):
                    pe.wait_ge(s_kv, i + 1)
                    at_least(pe, s_tk, i)
                    at_least(pe, s_tv, i)
                    pe.matmul(k_ps[:, :], kv_t[:, 0:P], ak[:, :, :].rearrange("p r c -> p (r c)"), start=True, stop=True)
                    pe.matmul(v_ps[:, :], kv_t[:, P:2 * P], am[:, :, :].rearrange("p r c -> p (r c)"),
                              start=True, stop=True).then_inc(s_tab, 1)

                def turn(new, old):
                    if new:
                        turn_inputs(*new)
                    if old:
                        project(*old[:2])
                    if new:
                        linear(*new[:2])
                    if old:
                        relate(*old[:2])

                over_tiles(pe, turn)


def mark_loads(from_x):
    return 16 * (1 + 3 + 1 + 3 * 4 + 2 * H + (0 if from_x else 3 + 1))


def final_phase(nc, dram, const):
    ph = Phase(nc, "final")
    with ph.stack:
        sb, ps, sem = ph.sb, ph.ps, ph.sem
        q, sums, ident = const["q"], const["sums"], const["ident"]
        PIECES = 7
        PT = TILES // PIECES
        w = sb("w", [P, TYPES, P])
        b, b16 = sb("b", [P, TYPES, P]), sb("b16", [P, TYPES, P], BF16)
        ones16 = sb("ones16", [P, P], BF16)
        skip_all, stay_all = sb("skip_all", [P, TYPES]), sb("stay_all", [P, TYPES])
        type_rows, mask, stay = sb("type_rows", [TILES, P]), sb("mask", [P, TYPES, TILES]), sb("stay", [P, TILES])
        h_old, h_tile = sb("h_old", [P, NP]), sb("h_tile", [P, 2, P])
        weight, recip = sb("weight", [P, H]), sb("recip", [P, H])
        mean_v, g, g_t = sb("mean_v", [P, 2, P]), sb("g", [P, 2, P]), sb("g_t", [P, 2, P])
        part = sb("part", [P, P])
        stats = sb("stats", [P, TILES, 6])
        both, apart, mean, spread, rstd, shift = (sb(n, [P, TILES]) for n in (
            "both", "apart", "mean", "spread", "rstd", "shift"))
        g_ps, old_ps, out_ps = ([ps(f"{n}{u}", [P, BANK]) for u in range(2)] for n in ("g_ps", "old_ps", "out_ps"))
        s_set, s_w, s_v, s_skip, s_rows, s_type = (sem(n) for n in ("s_set", "s_w", "s_v", "s_skip", "s_rows", "s_type"))
        s_piece = [sem(f"s_piece{c}") for c in range(PIECES)]
        s_loaded, s_tile, s_weight, s_recip, s_mean, s_g, s_gt = (
            sem(n) for n in ("s_loaded", "s_tile", "s_weight", "s_recip", "s_mean", "s_g", "s_gt"))
        s_turned, s_old, s_lin, s_part, s_stats, s_root = (
            sem(n) for n in ("s_turned", "s_old", "s_lin", "s_part", "s_stats", "s_root"))
        s_end_dve, s_end_act, s_out = sem("s_end_dve"), sem("s_end_act"), sem("s_out")
        mark = {}
        ENDS = 7
        HALF = TILES // 2

        def over_tiles(engine, turn):
            turn(0, 0)
            turn(1, 1)
            with engine.Fori(1, TILES // 2 - 2) as k:
                turn(k * 2, 0)
                turn(k * 2 + 1, 1)
            for i in range(TILES - 4, TILES):
                turn(i, i % 2)

        def beyond(i):
            return isinstance(i, int) and i >= TILES

        def tile_of(buffer, i):
            return buffer[:, bass.ds(i, 1), :].rearrange("p o c -> p (o c)")

        with nc.Block() as block:
            @block.vector
            def _(dve):
                count = [0]

                def then(instruction):
                    count[0] += 1
                    instruction.then_inc(s_v, 1)
                    dve.wait_ge(s_v, count[0])

                def weigh(i):
                    if not beyond(i):
                        at_least(dve, s_recip, i)
                        one = sums[:, bass.ds(i + 1, 1), :].rearrange("p o (h c) -> p (o h) c", c=HW)
                        dve.tensor_scalar(weight[:, :], one[:, :, DH], 1e-16, None, ALU.add).then_inc(s_weight, 1)

                def invert(i):
                    if not beyond(i):
                        dve.wait_ge(s_weight, i + 1)
                        at_least(dve, s_mean, i)
                        dve.reciprocal(recip[:, :], weight[:, :]).then_inc(s_recip, 1)

                def divide(i, u):
                    if not beyond(i):
                        one = sums[:, bass.ds(i + 1, 1), :].rearrange("p o (h c) -> p (o h) c", c=HW)
                        dve.wait_ge(s_recip, i + 1)
                        at_least(dve, s_g, i - 1)
                        dve.tensor_tensor(mean_v[:, u, :].rearrange("p (h c) -> p h c", c=DH), one[:, :, 0:DH],
                                          recip[:, :].unsqueeze(2).broadcast_to([P, H, DH]), ALU.mult).then_inc(s_mean, 1)

                def pick(i, u, t, to, added):
                    dve.scalar_tensor_tensor(out=to, in0=out_ps[u][:, t * P:(t + 1) * P], scalar=mask[:, t, bass.ds(i, 1)],
                                             in1=added, op0=ALU.mult, op1=ALU.add).then_inc(s_part, 1)

                def turn(i, u):
                    dve.wait_ge(s_lin, i + 1)
                    dve.wait_ge(s_old, i + 1)
                    dve.wait_ge(s_loaded, i + 1)
                    at_least(dve, s_part, i * 4)
                    pick(i, u, 0, part[:, :], tile_of(q, i))
                    if not (isinstance(i, int) and i == 0):
                        dve.bn_stats(stats[:, bass.ds(i - 1, 1), :].rearrange("p o c -> p (o c)"),
                                     tile_of(q, i - 1)).then_inc(s_stats, 1)
                    dve.wait_ge(s_part, i * 4 + 1)
                    pick(i, u, 1, part[:, :], part[:, :])
                    weigh(i + 3)
                    dve.wait_ge(s_part, i * 4 + 2)
                    pick(i, u, 2, part[:, :], part[:, :])
                    invert(i + 3)
                    dve.wait_ge(s_part, i * 4 + 3)
                    dve.scalar_tensor_tensor(out=tile_of(q, i), in0=old_ps[u][:, 0:P], scalar=stay[:, bass.ds(i, 1)],
                                             in1=part[:, :], op0=ALU.mult, op1=ALU.add).then_inc(s_part, 1)
                    divide(i + 3, 1 - u)

                dve.memset(b[:, :, :], 0.0).then_inc(s_set, 1)
                dve.memset(ones16[:, :], 1.0).then_inc(s_set, 1)
                for i in range(3):
                    weigh(i)
                    invert(i)
                    divide(i, i % 2)
                dve.wait_ge(s_skip, 1)
                for t in range(TYPES):
                    then(dve.tensor_scalar(w[:, t, :], w[:, t, :], skip_all[:, t:t + 1], None, ALU.mult))
                    then(dve.tensor_scalar(b[:, t, :], b[:, t, :], skip_all[:, t:t + 1], None, ALU.mult))
                split_in_three(dve, then, b[:, :, :], b16[:, :, :])
                then(dve.tensor_scalar(stay_all[:, :], skip_all[:, :], -1.0, 1.0, ALU.mult, ALU.add))
                dve.wait_ge(s_type, 1)
                for t in range(TYPES):
                    then(dve.tensor_scalar(mask[:, t, :], out_ps[1][:, 0:TILES], float(t), None, ALU.is_equal))
                mark["types"] = count[0]
                then(dve.tensor_scalar(stay[:, :], mask[:, 0, :], stay_all[:, 0:1], None, ALU.mult))
                for t in (1, 2):
                    then(dve.scalar_tensor_tensor(out=stay[:, :], in0=mask[:, t, :], scalar=stay_all[:, t:t + 1],
                                                  in1=stay[:, :], op0=ALU.mult, op1=ALU.add))
                over_tiles(dve, turn)
                dve.wait_ge(s_part, TILES * 4)
                dve.bn_stats(stats[:, TILES - 1, :], q[:, TILES - 1, :]).then_inc(s_stats, 1)

                dve.wait_ge(s_stats, TILES)
                dve.tensor_tensor(both[:, :], stats[:, :, 1], stats[:, :, 4], ALU.add)
                dve.tensor_tensor(apart[:, :], stats[:, :, 1], stats[:, :, 4], ALU.subtract)
                then(dve.tensor_tensor(spread[:, :], stats[:, :, 2], stats[:, :, 5], ALU.add))
                dve.tensor_scalar(mean[:, :], both[:, :], 0.5, None, ALU.mult)
                then(dve.scalar_tensor_tensor(out=apart[:, :], in0=apart[:, :], scalar=0.25, in1=apart[:, :],
                                              op0=ALU.mult, op1=ALU.mult))
                then(dve.scalar_tensor_tensor(out=spread[:, :], in0=spread[:, :], scalar=1.0 / D, in1=apart[:, :],
                                              op0=ALU.mult, op1=ALU.add))
                then(dve.tensor_scalar(spread[:, :], spread[:, :], EPS, None, ALU.add))
                mark["spread"] = count[0]
                dve.wait_ge(s_root, 1)
                then(dve.reciprocal(rstd[:, :], rstd[:, :]))
                then(dve.scalar_tensor_tensor(out=shift[:, :], in0=mean[:, :], scalar=-1.0, in1=rstd[:, :],
                                              op0=ALU.mult, op1=ALU.mult))
                mark["shift"] = count[0]
                with dve.Fori(0, HALF // ENDS) as k:
                    for i in (k * ENDS + j for j in range(ENDS)):
                        dve.tensor_scalar(tile_of(q, i), tile_of(q, i), rstd[:, bass.ds(i, 1)],
                                          shift[:, bass.ds(i, 1)], ALU.mult, ALU.add).then_inc(s_end_dve, 1)

            @block.scalar
            def _(act):
                def gelu(i, u):
                    if not beyond(i):
                        act.wait_ge(s_mean, i + 1)
                        at_least(act, s_turned, i - 1)
                        act.activation(g[:, u, :], mean_v[:, u, :], ACT.Gelu_apprx_tanh).then_inc(s_g, 1)

                def turn(i, u):
                    act.wait_ge(s_turned, i + 1)
                    at_least(act, s_lin, i - 1)
                    act.activation(g_t[:, u, :], g_ps[u][:, 0:P], ACT.Copy).then_inc(s_gt, 1)
                    gelu(i + 2, u)

                act.wait_ge(s_w, 16 * 5)
                act.activation(skip_all[:, :], skip_all[:, :], ACT.Sigmoid).then_inc(s_skip, 1)
                gelu(0, 0)
                gelu(1, 1)
                over_tiles(act, turn)
                act.wait_ge(s_v, mark["spread"])
                act.activation(rstd[:, :], spread[:, :], ACT.Sqrt).then_inc(s_root, 1)
                act.wait_ge(s_v, mark["shift"])
                with act.Fori(0, HALF // ENDS) as k:
                    for i in (k * ENDS + (HALF + j) for j in range(ENDS)):
                        act.activation(tile_of(q, i), tile_of(q, i), ACT.Identity, bias=shift[:, bass.ds(i, 1)],
                                       scale=rstd[:, bass.ds(i, 1)]).then_inc(s_end_act, 1)

            @block.gpsimd
            def _(pool):
                def turn(i, u):
                    pool.wait_ge(s_loaded, i + 1)
                    at_least(pool, s_old, i - 1)
                    pool.tensor_copy(h_tile[:, u, :], h_old[:, bass.ds(i * P, P)]).then_inc(s_tile, 1)

                over_tiles(pool, turn)

            @block.sync
            def _(sp):
                sp.dma_start(w[:, :, :], dram["Wa"][LAYERS - 1].rearrange("t i o -> i t o")).then_inc(s_w, 16)
                sp.dma_start(skip_all[:, :], dram["skip"][LAYERS - 1].unsqueeze(0).broadcast_to([P, TYPES])).then_inc(s_w, 16)
                sp.dma_start(type_rows[:, :], dram["type_f"].rearrange("(m p) -> m p", p=P)).then_inc(s_rows, 16)
                sp.wait_ge(s_set, 1)
                for at in (0, 32, 64):
                    sp.dma_start(b[at:at + 1, :, :], dram["ba"][LAYERS - 1].unsqueeze(0)).then_inc(s_w, 16)
                for c in range(PIECES):
                    first, whole = c * PT, min((c + 1) * PT, N // P)
                    sp.dma_start(h_old[:, first * P:(c + 1) * PT * P],
                                 dram["h_t"][LAYERS - 1][:, first * P:(c + 1) * PT * P]).then_inc(s_piece[c], 16)
                    sp.dma_start(q[:, first:whole, :],
                                 dram["x"][first * P:whole * P, :].rearrange("(m p) c -> p m c", p=P)).then_inc(s_piece[c], 16)
                sp.dma_start(q[0:N % P, TILES - 1, :], dram["x"][N - N % P:N, :]).then_inc(s_piece[PIECES - 1], 16)
                for c in range(PIECES):
                    sp.wait_ge(s_piece[c], 48 if c == PIECES - 1 else 32)
                    sp.sem_inc(s_loaded, PT)
                step = -(-HALF // 4)
                for first in range(0, HALF, step):
                    for base, s_end in ((0, s_end_dve), (HALF, s_end_act)):
                        start, stop = base + first, base + min(first + step, HALF)
                        sp.wait_ge(s_end, stop - base)
                        whole = min(stop, N // P)
                        sp.dma_start(dram["out"][start * P:whole * P, :].rearrange("(m p) c -> p m c", p=P),
                                     q[:, start:whole, :]).then_inc(s_out, 16)
                sp.dma_start(dram["out"][N - N % P:N, :], q[0:N % P, TILES - 1, :]).then_inc(s_out, 16)
                sp.wait_ge(s_out, 16 * (2 * len(range(0, HALF, step)) + 1))

            @block.tensor
            def _(pe):
                def turn_gelu(i, u):
                    if not beyond(i):
                        pe.wait_ge(s_g, i + 1)
                        at_least(pe, s_gt, i - 1)
                        pe.transpose(g_ps[u][:, 0:P], g[:, u, :], ident[:, :]).then_inc(s_turned, 1)

                def turn_old(i, u):
                    if not beyond(i):
                        pe.wait_ge(s_tile, i + 1)
                        at_least(pe, s_part, (i - 1) * 4)
                        pe.transpose(old_ps[u][:, 0:P], h_tile[:, u, :], ident[:, :]).then_inc(s_old, 1)

                def turn(i, u):
                    turn_gelu(i + 1, 1 - u)
                    pe.wait_ge(s_gt, i + 1)
                    at_least(pe, s_part, (i - 1) * 4)
                    pe.matmul(out_ps[u][:, 0:TYPES * P], g_t[:, u, :], w[:, :, :].rearrange("p t c -> p (t c)"),
                              start=True, stop=False)
                    pe.matmul(out_ps[u][:, 0:TYPES * P], ones16[:, :], b16[:, :, :].rearrange("p t c -> p (t c)"),
                              start=False, stop=True).then_inc(s_lin, 1)
                    turn_old(i + 1, 1 - u)

                pe.wait_ge(s_rows, 16)
                pe.transpose(out_ps[1][:, 0:TILES], type_rows[:, :], ident[0:TILES, 0:TILES]).then_inc(s_type, 1)
                turn_old(0, 0)
                turn_gelu(0, 0)
                pe.wait_ge(s_v, mark["types"])
                over_tiles(pe, turn)


def edge_phase(nc, dram, const, layer):
    ph = Phase(nc, f"edge{layer}")
    with ph.stack:
        sb, ps = ph.sb, ph.ps
        q, sums, ident, ident16 = (const[n] for n in ("q", "sums", "ident", "ident16"))
        gather_rows, local = sb("gather_rows", [P, 2, SPB], I32), sb("local", [P, 2, SPB], BF16)
        info_ahead, info_behind = sb("info_ahead", [1, 2, SPB], I32), sb("info_behind", [1, 2, 4, SPB], I32)
        links = sb("links", [P, P + 1])
        runs_fwd, runs_bwd = sb("runs_fwd", [1, H, SPB + 1]), sb("runs_bwd", [1, H, SPB + 1])
        kv = sb("kv", [P, 2, SPB, 2 * D])
        onehot = sb("onehot", [P, 2, SPB, P], BF16)
        spread = sb("spread", [P, 2, SPG, P])
        products = sb("products", [P, SPG, P])
        logits = sb("logits", [P, 2, H, SPB])
        scan_a, scan_b = sb("scan_a", [P, P]), sb("scan_b", [P, P])
        ends_fwd, ends_bwd = sb("ends_fwd", [1, H, SPB + 1]), sb("ends_bwd", [1, H, SPB + 1])
        carry_fwd, carry_bwd = sb("carry_fwd", [1, H, SPB + 1]), sb("carry_bwd", [1, H, SPB + 1])
        carry_rows, carry_cols = sb("carry_rows", [1, 2, P]), sb("carry_cols", [P, 2])
        first_max, drop, linked = sb("first_max", [1, H]), sb("drop", [1, H]), sb("linked", [1, 1])
        first_hot, first_cold = sb("first_hot", [1, P]), sb("first_cold", [1, P])
        below, exps = scan_a, scan_b
        keep_share = sb("keep_share", [1, H])
        weights = sb("weights", [P, H, SPB])
        scale, rescaled = sb("scale", [P, H]), sb("rescaled", [P, AW])
        hot32 = sb("hot32", [P, 2, SPG, P])
        weighted = sb("weighted", [P, 2, SPG, AW])
        slot_ps = ph.ps("slot_ps", [P, (SLOTS + 1) * BANK])
        q_ps = ph.ps("q_ps", [P, 2, SPG, P])
        turn_ps = ph.ps("turn_ps", [P, SPG, P], BF16)
        logit_ps = ph.ps("logit_ps", [P, BANK])
        exp_ps = logit_ps[:, P:2 * P]
        row_ps = logit_ps[0:1, P:3 * P]
        col_ps = logit_ps[:, 3 * P:3 * P + 2]
        scale_ps = logit_ps[:, 3 * P + 4:3 * P + 4 + H]

        s_scan, s_pause = ph.sem("s_scan"), ph.sem("s_pause")
        s_plan, s_behind = ([ph.sem(f"{n}{u}") for u in range(2)] for n in ("s_plan", "s_behind"))
        s_kv = [[ph.sem(f"s_kv{u}_{g}") for g in range(GPB)] for u in range(2)]
        (s_set, s_hot, s_hot_t, s_spread, s_q, s_prod, s_logit, s_logit_t, s_ends, s_row, s_chain, s_carry, s_col,
         s_colcopy, s_half, s_below, s_exp, s_exp_t, s_weight, s_scaled, s_hot32, s_weighted, s_step, s_copied) = (
            ph.sem(n) for n in (
                "s_set", "s_hot", "s_hot_t", "s_spread", "s_q", "s_prod", "s_logit", "s_logit_t", "s_ends",
                "s_row", "s_chain", "s_carry", "s_col", "s_colcopy", "s_half", "s_below", "s_exp", "s_exp_t", "s_weight",
                "s_scaled", "s_hot32", "s_weighted", "s_step", "s_copied"))
        SUM_GROUPS = [[], [0], [1], [2], [3, 4], [5], [6], [7]]
        CHAIN = 5

        def bodies(engine, body):
            body(0, 0, 0, True, False)
            for b in (1, 2, 3):
                body(b, b % 2, b // 2, True, True)
            with engine.Fori(2, BLOCKS // 2 - 1) as k:
                body(k * 2, 0, k, True, True)
                body(k * 2 + 1, 1, k, True, True)
            for b in (BLOCKS - 2, BLOCKS - 1):
                body(b, b % 2, b // 2, True, True)
            body(BLOCKS, 0, BLOCKS // 2, False, True)

        def pick(engine, ap, high):
            return nc.values_load_multi_w_load_instructions(
                ap, engines=[engine.engine], min_val=0, max_val=high, skip_runtime_bounds_check_because=WHY)[1]

        def pause(engine):
            engine.sem_inc(s_pause, 1)

        with nc.Block() as block:
            @block.sync
            def _(sp):
                def rows_of(b, u):
                    steps = bass.ds(b * SPB, SPB)
                    at_least(sp, s_prod, (b - 1) * GPB)
                    at_least(sp, s_hot, (b - 1) * GPB)
                    sp.dma_start(gather_rows[:, u, :], dram["rows_t"][:, steps]).then_inc(s_plan[u], 16)
                    sp.dma_start(local[:, u, :], dram["local_t"][:, steps]).then_inc(s_plan[u], 16)
                    sp.dma_start(info_ahead[:, u, :], dram["info"][0, steps].unsqueeze(0)).then_inc(s_plan[u], 16)

                def sums_of(b, u):
                    steps = bass.ds(b * SPB, SPB)
                    at_least(sp, s_copied, (b - 1) * SPB)
                    at_least(sp, s_step, (b - 1) * SPB)
                    sp.dma_start(info_behind[:, u, :, :], dram["info"][1:5, steps].unsqueeze(0)).then_inc(s_behind[u], 16)

                def links_of(b):
                    steps = bass.ds(b * SPB, SPB)
                    at_least(sp, s_below, b)
                    for hd in range(H):
                        sp.dma_start(links[hd * SPB:(hd + 1) * SPB, :], dram_ap(
                            dram["link"], b * (SPB * P), [[P, SPB], [1, P + 1]])).then_inc(s_scan, 16)
                    for to, name, at in ((runs_fwd, "run_fwd", 1), (runs_bwd, "run_bwd", 0)):
                        sp.dma_start(to[:, :, at:at + SPB], dram[name][steps].unsqueeze(0).unsqueeze(0).broadcast_to(
                            [1, H, SPB])).then_inc(s_scan, 16)

                rows_of(0, 0)
                rows_of(1, 1)
                sums_of(0, 0)
                sp.wait_ge(s_set, 4)
                links_of(0)
                with sp.Fori(1, BLOCKS // 2) as k:
                    for u in range(2):
                        rows_of(k * 2 + u, u)
                        sums_of(k * 2 + (u - 1), 1 - u)
                        links_of(k * 2 + (u - 1))
                sums_of(BLOCKS - 1, 1)
                links_of(BLOCKS - 1)

            @block.gpsimd
            def _(pool):
                def body(b, u, k, ahead, behind):
                    if not ahead:
                        return
                    for g in range(GPB):
                        if g == 0:
                            pool.wait_ge(s_plan[u], (k + 1) * 48)
                        at_least(pool, s_weighted, (b - 2) * GPB + (g + 1))
                        pause(pool)
                        for j in range(SPG):
                            s = g * SPG + j
                            pool.indirect_dma_start(kv[:, u, s, :], None, dram["table"][layer],
                                                    bass.IndirectOffsetOnAxis(ap=gather_rows[:, u, s:s + 1], axis=0)
                                                    ).then_inc(s_kv[u][g], 16)

                bodies(pool, body)

            @block.vector
            def _(dve):
                for to in (ends_fwd[:, :, 0:1], ends_bwd[:, :, SPB:SPB + 1], runs_fwd[:, :, 0:1],
                           runs_bwd[:, :, SPB:SPB + 1]):
                    dve.memset(to, -BIG).then_inc(s_set, 1)

                def one_hot(b, u, k, g):
                    if g == 0:
                        dve.wait_ge(s_plan[u], (k + 1) * 48)
                    at_least(dve, s_hot32, (b - 2) * GPB + (g + 1))
                    at_least(dve, s_hot_t, (b - 2) * GPB + (g + 1))
                    shape = [P, SPG, P]
                    dve.tensor_tensor(onehot[:, u, g * SPG:(g + 1) * SPG, :], const["column16"][:, :].unsqueeze(1).broadcast_to(shape),
                                      local[:, u, g * SPG:(g + 1) * SPG].unsqueeze(2).broadcast_to(shape),
                                      ALU.is_equal).then_inc(s_hot, 1)

                def multiply(b, u, k, g):
                    dve.wait_ge(s_kv[u][g], (k + 1) * (16 * SPG))
                    dve.wait_ge(s_q, b * GPB + (g + 1))
                    at_least(dve, s_logit, b * GPB + g)
                    dve.tensor_tensor(products[:, :, :], q_ps[:, g % 2, :, :], kv[:, u, g * SPG:(g + 1) * SPG, 0:D],
                                      ALU.mult).then_inc(s_prod, 1)

                def add_up(b, u, k, g):
                    dve.wait_ge(s_prod, b * GPB + (g + 1))
                    if g == 0:
                        at_least(dve, s_logit_t, b - 1)
                    dve.tensor_reduce(logits[:, u, :, g * SPG:(g + 1) * SPG].rearrange("p h s -> p s h"),
                                      products[:, :, :].rearrange("p s (h c) -> p s h c", c=DH),
                                      AX.X, ALU.add).then_inc(s_logit, 1)

                def row_ends(b, w, kw):
                    dve.wait_ge(s_scan, b * (16 * (H + 2)))
                    dve.wait_ge(s_logit_t, b)
                    at_least(dve, s_row, b - 1)
                    dve.tensor_tensor_scan(scan_a[:, :], links[:, 0:P], logit_ps[:, 0:P], -BIG, ALU.add, ALU.max)
                    dve.tensor_tensor_scan(scan_b[:, ::-1], links[:, 1:P + 1][:, ::-1], logit_ps[:, 0:P][:, ::-1], -BIG,
                                           ALU.add, ALU.max).then_inc(s_ends, 1)

                def carries(b, w, kw):
                    base = (b - 1) * CHAIN
                    at = [0]

                    def then(*instructions):
                        at[0] += 1
                        instructions[-1].then_inc(s_chain, 1)
                        dve.wait_ge(s_chain, base + at[0])

                    rows = row_ps.rearrange("o (w h s) -> o w h s", w=2, h=H)
                    flat = lambda ap: ap.rearrange("o h s -> o (h s)")
                    dve.wait_ge(s_set, 4)
                    dve.wait_ge(s_row, b)
                    at_least(dve, s_exp_t, b - 1)
                    then(dve.tensor_copy(ends_fwd[:, :, 1:SPB + 1], rows[:, 0, :, :]),
                         dve.tensor_copy(ends_bwd[:, :, 0:SPB], rows[:, 1, :, :]),
                         dve.tensor_copy(first_hot[:, :], onehot[0:1, w, 0, :]))
                    at_least(dve, s_col, b - 1)
                    at_least(dve, s_exp, b - 1)
                    then(dve.tensor_tensor_scan(flat(carry_fwd[:, :, :]), flat(runs_fwd[:, :, :]), flat(ends_fwd[:, :, :]),
                                                -BIG, ALU.add, ALU.max),
                         dve.tensor_tensor_scan(flat(carry_bwd[:, :, :])[:, ::-1], flat(runs_bwd[:, :, :])[:, ::-1],
                                                flat(ends_bwd[:, :, :])[:, ::-1], -BIG, ALU.add, ALU.max),
                         dve.tensor_scalar(first_cold[:, :], first_hot[:, :], -1.0, 1.0, ALU.mult, ALU.add),
                         dve.tensor_scalar(linked[:, :], links[0:1, 0:1], -1.0, None, ALU.is_ge))
                    then(dve.tensor_copy(carry_rows[:, 0, :].rearrange("o (h s) -> o h s", h=H), carry_fwd[:, :, 0:SPB]),
                         dve.tensor_copy(carry_rows[:, 1, :].rearrange("o (h s) -> o h s", h=H), carry_bwd[:, :, 1:SPB + 1]),
                         dve.tensor_tensor(first_max[:, :], ends_fwd[:, :, 0], carry_bwd[:, :, 0], ALU.max))
                    then(dve.tensor_tensor(drop[:, :], ends_fwd[:, :, 0], first_max[:, :], ALU.subtract))
                    then(dve.tensor_copy(ends_fwd[:, :, 0], carry_fwd[:, :, SPB]))
                    assert at[0] == CHAIN

                def maxima(b, w):
                    dve.wait_ge(s_col, b)
                    dve.tensor_copy(carry_cols[:, :], col_ps).then_inc(s_colcopy, 1)
                    dve.wait_ge(s_colcopy, b)
                    dve.tensor_tensor_scan(scan_a[:, :], links[:, 0:P], logit_ps[:, 0:P], carry_cols[:, 0:1],
                                           ALU.add, ALU.max).then_inc(s_half, 1)
                    dve.wait_ge(s_half, b * 2 - 1)
                    dve.tensor_tensor_scan(scan_b[:, ::-1], links[:, 1:P + 1][:, ::-1], scan_a[:, ::-1], carry_cols[:, 1:2],
                                           ALU.add, ALU.max).then_inc(s_half, 1)
                    dve.wait_ge(s_half, b * 2)
                    dve.tensor_tensor(below[:, :], logit_ps[:, 0:P], scan_b[:, :], ALU.subtract).then_inc(s_below, 1)

                def back_to_edges(b, slot):
                    dve.wait_ge(s_exp_t, b)
                    dve.tensor_copy(weights[:, :, :], exp_ps.rearrange("p (h s) -> p h s", h=H)).then_inc(s_weight, 1)
                    dve.tensor_copy(scale[:, :], scale_ps).then_inc(s_weight, 1)
                    dve.wait_ge(s_weight, b * 2)
                    at_least(dve, s_step, (b - 1) * SPB)
                    dve.tensor_tensor(rescaled[:, :].rearrange("p (h c) -> p h c", c=HW),
                                      slot_ps[:, bass.ds(slot, AW)].rearrange("p (h c) -> p h c", c=HW),
                                      scale[:, :].unsqueeze(2).broadcast_to([P, H, HW]), ALU.mult).then_inc(s_scaled, 1)

                def weigh(b, w, c):
                    done = (b - 1) * GPB + c
                    if c == 0:
                        dve.wait_ge(s_weight, b * 2)
                    at_least(dve, s_step, (done - 1) * SPG)
                    steps = slice(c * SPG, (c + 1) * SPG)
                    to = weighted[:, c % 2, :, :].rearrange("p s (h c) -> p s h c", c=HW)
                    share = weights[:, :, steps].rearrange("p h s -> p s h")
                    dve.tensor_tensor(to[:, :, :, 0:DH], kv[:, w, steps, D:2 * D].rearrange("p s (h c) -> p s h c", c=DH),
                                      share.unsqueeze(3).broadcast_to([P, SPG, H, DH]), ALU.mult)
                    dve.tensor_copy(to[:, :, :, DH], share).then_inc(s_weighted, 1)

                one_hot(0, 0, 0, 0)

                def body(b, u, k, ahead, behind):
                    w, kw = 1 - u, k if u else k - 1
                    if behind and not ahead:
                        dve.wait_ge(s_logit, b * GPB)
                    for g in range(GPB):
                        if behind and g == 0:
                            row_ends(b, w, kw)
                        if ahead:
                            if g < GPB - 1:
                                one_hot(b, u, k, g + 1)
                            elif not (isinstance(b, int) and b == BLOCKS - 1):
                                one_hot(b + 1, 1 - u, k + 1 if u else k, 0)
                        if behind and g == 0:
                            dve.wait_ge(s_behind[w], (kw + 1) * 16)
                            pause(dve)
                            slot, = pick(dve, info_behind[0:1, w, 0, 0:1], (SLOTS - 1) * BANK)
                            carries(b, w, kw)
                        if behind and g == 1:
                            back_to_edges(b, slot)
                        for c in SUM_GROUPS[g] if behind else ():
                            weigh(b, w, c)
                        if ahead:
                            multiply(b, u, k, g)
                        if behind and g == 0:
                            maxima(b, w)
                        if ahead:
                            add_up(b, u, k, g)

                bodies(dve, body)

            @block.scalar
            def _(act):
                def spread_copy(b, u, k, g):
                    act.wait_ge(s_hot_t, b * GPB + (g + 1))
                    at_least(act, s_q, b * GPB + (g - 1))
                    act.activation(spread[:, g % 2, :, :], turn_ps[:, :, :], ACT.Copy).then_inc(s_spread, 1)

                def widen(b, w, c):
                    done = (b - 1) * GPB + c
                    at_least(act, s_step, (done - 1) * SPG)
                    act.activation(hot32[:, c % 2, :, :], onehot[:, w, c * SPG:(c + 1) * SPG, :], ACT.Copy).then_inc(s_hot32, 1)

                def keep_finished(b, w, kw, c):
                    numbers = pick(act, info_behind[0:1, w, 2:4, c * SPG:(c + 1) * SPG], (TILES + 1) * AW)
                    others = [nc.s_assert_within(n, 0, (SLOTS - 1) * BANK, skip_runtime_bounds_check_because=WHY)
                              for n in numbers[:SPG]]
                    places = numbers[SPG:]
                    for j, (other, place) in enumerate(zip(others, places)):
                        s = c * SPG + j
                        at_least(act, s_step, (b - 1) * SPB + s)
                        at_least(act, s_copied, (b - 1) * SPB + (s - 1))
                        act.activation(sums[:, :, :].rearrange("p t c -> p (t c)")[:, bass.ds(place, AW)],
                                       slot_ps[:, bass.ds(other, AW)], ACT.Copy).then_inc(s_copied, 1)

                def body(b, u, k, ahead, behind):
                    w, kw = 1 - u, k if u else k - 1
                    for g in range(GPB):
                        if behind and g == 1:
                            act.wait_ge(s_behind[w], (kw + 1) * 16)
                            pause(act)
                            act.wait_ge(s_below, b)
                            at_least(act, s_exp_t, b - 1)
                            act.activation(exps[:, :], below[:, :], ACT.Exp)
                            act.wait_ge(s_chain, b * CHAIN)
                            act.activation(keep_share[:, :], drop[:, :], ACT.Exp, scale=linked[:, :]).then_inc(s_exp, 1)
                        for c in SUM_GROUPS[g] if behind else ():
                            widen(b, w, c)
                        if ahead:
                            if g < GPB - 1:
                                spread_copy(b, u, k, g + 1)
                            elif not (isinstance(b, int) and b == BLOCKS - 1):
                                spread_copy(b + 1, 1 - u, k + 1 if u else k, 0)
                        for c in SUM_GROUPS[g] if behind else ():
                            keep_finished(b, w, kw, c)

                spread_copy(0, 0, 0, 0)
                bodies(act, body)
                act.wait_ge(s_step, STEPS)
                act.wait_ge(s_copied, STEPS)
                act.activation(sums[:, TILES, :], slot_ps[:, ((TILES - 1) % SLOTS) * BANK:((TILES - 1) % SLOTS) * BANK + AW], ACT.Copy)

            @block.tensor
            def _(pe):
                zeros = const["zero16"]
                for slot in range(SLOTS):
                    pe.matmul(slot_ps[:, slot * BANK:slot * BANK + AW], zeros[:, 0:P], zeros[:, :], start=True, stop=True)

                def turn_hot(b, u, k, g):
                    pe.wait_ge(s_hot, b * GPB + (g + 1))
                    at_least(pe, s_spread, b * GPB + g)
                    for j in range(SPG):
                        last = pe.transpose(turn_ps[:, j, :], onehot[:, u, g * SPG + j, :], ident16[:, :])
                    last.then_inc(s_hot_t, 1)

                def spread_q(b, u, k, g):
                    if g == 0:
                        pe.wait_ge(s_plan[u], (k + 1) * 48)
                        pause(pe)
                    columns = pick(pe, info_ahead[0:1, u, g * SPG:(g + 1) * SPG], (TILES - 1) * P)
                    pe.wait_ge(s_spread, b * GPB + (g + 1))
                    at_least(pe, s_prod, b * GPB + (g - 1))
                    for j in range(SPG):
                        last = pe.matmul(q_ps[:, g % 2, j, :], spread[:, g % 2, j, :],
                                         q[:, :, :].rearrange("p t c -> p (t c)")[:, bass.ds(columns[j], P)], start=True, stop=True)
                    last.then_inc(s_q, 1)

                def add_group(b, w, kw, c):
                    numbers = pick(pe, info_behind[0:1, w, 0:2, c * SPG:(c + 1) * SPG], SLOTS * BANK)
                    slots, clears = numbers[:SPG], numbers[SPG:]
                    pe.wait_ge(s_weighted, (b - 1) * GPB + (c + 1))
                    pe.wait_ge(s_hot32, (b - 1) * GPB + (c + 1))
                    for j in range(SPG):
                        s = c * SPG + j
                        at_least(pe, s_copied, (b - 1) * SPB + (s - 1))
                        pe.matmul(slot_ps[:, bass.ds(clears[j], AW)], zeros[:, 0:P], zeros[:, :], start=True, stop=True)
                        pe.matmul(slot_ps[:, bass.ds(slots[j], AW)], hot32[:, c % 2, j, :], weighted[:, c % 2, j, :],
                                  start=False, stop=True, skip_group_check=True).then_inc(s_step, 1)

                def body(b, u, k, ahead, behind):
                    w, kw = 1 - u, k if u else k - 1
                    for g in range(GPB):
                        if behind and g == 0:
                            pe.wait_ge(s_logit, b * GPB)
                            at_least(pe, s_weight, (b - 1) * 2)
                            pe.transpose(logit_ps[:, 0:P], logits[:, w, :, :].rearrange("p h s -> p (h s)"),
                                         ident[:, :]).then_inc(s_logit_t, 1)
                            pe.wait_ge(s_ends, b)
                            at_least(pe, s_chain, (b - 1) * CHAIN)
                            pe.transpose(row_ps[:, 0:P], scan_a[:, P - 1:P], ident[:, :])
                            pe.transpose(row_ps[:, P:2 * P], scan_b[:, 0:1], ident[:, :]).then_inc(s_row, 1)
                        if ahead:
                            spread_q(b, u, k, g)
                            if g < GPB - 1:
                                turn_hot(b, u, k, g + 1)
                            elif not (isinstance(b, int) and b == BLOCKS - 1):
                                turn_hot(b + 1, 1 - u, k + 1 if u else k, 0)
                        if not behind:
                            continue
                        if g == 0:
                            pe.wait_ge(s_chain, b * CHAIN)
                            at_least(pe, s_colcopy, b - 1)
                            pause(pe)
                            pe.transpose(col_ps[:, 0:1], carry_rows[:, 0, :], ident[0:1, 0:1])
                            pe.transpose(col_ps[:, 1:2], carry_rows[:, 1, :], ident[0:1, 0:1]).then_inc(s_col, 1)
                        if g == 1:
                            pe.wait_ge(s_exp, b)
                            at_least(pe, s_weight, (b - 1) * 2)
                            pe.transpose(exp_ps, exps[:, :], ident[:, :])
                            pe.matmul(scale_ps, first_hot[:, :], keep_share[:, :], start=True, stop=False)
                            pe.matmul(scale_ps, first_cold[:, :], const["ones"][0:1, 0:H], start=False,
                                      stop=True).then_inc(s_exp_t, 1)
                            pe.wait_ge(s_behind[w], (kw + 1) * 16)
                            pause(pe)
                            slot, = pick(pe, info_behind[0:1, w, 0, 0:1], (SLOTS - 1) * BANK)
                            pe.wait_ge(s_scaled, b)
                            at_least(pe, s_copied, (b - 1) * SPB)
                            pe.matmul(slot_ps[:, bass.ds(slot, AW)], ident[:, :], rescaled[:, :], start=True, stop=True)
                        for c in SUM_GROUPS[g]:
                            add_group(b, w, kw, c)

                turn_hot(0, 0, 0, 0)
                bodies(pe, body)



def build_program(nc, args, out):
    def scratch(name, shape, dtype=F32):
        return nc.dram_tensor(f"scratch_{name}", shape, dtype).ap()

    dram = {
        "x": args["x"], "src": args["src"], "dst": args["dst"], "edge_type": args["edge_type_4"],
        "node_type": args["node_type_3"], "out": out,
        "edge_row": scratch("edge_row", [SK * P, P]), "edge_dst": scratch("edge_dst", [SK * P, P]),
        "type_f": scratch("type_f", [NP]), "key": scratch("key", [1 + STEPS * P]),
        "link": scratch("link", [(STEPS + 1) * P]), "run_fwd": scratch("run_fwd", [STEPS]),
        "run_bwd": scratch("run_bwd", [STEPS]), "info": scratch("info", [5, STEPS], I32),
        "rows_t": scratch("rows_t", [P, STEPS], I32), "local_t": scratch("local_t", [P, STEPS], BF16),
        "h_t": scratch("h_t", [2, P, NP]),
        "table": [scratch(f"table{layer}", [RELS * NP, 2 * D]) for layer in range(LAYERS)],
    }
    dram["edge_row_flat"] = dram["edge_row"].rearrange("c e -> (c e)")
    dram["edge_dst_flat"] = dram["edge_dst"].rearrange("c e -> (c e)")
    for short in ("W_in", "b_in", "Wk", "bk", "Wq", "bq", "Wv", "bv", "Wa", "ba", "a_rel", "m_rel", "mu", "skip"):
        dram[short] = args[f"L0_gnn_{short}"]

    keep = Phase(nc, "keep")
    with keep.stack:
        const = {
            "ident": keep.sb("ident", [P, P]), "ident16": keep.sb("ident16", [P, P], BF16),
            "ones": keep.sb("ones", [P, P]), "zero16": keep.sb("zero16", [32, AW], BF16),
            "column16": keep.sb("column16", [P, P], BF16),
            "q": keep.sb("q", [P, TILES, D]), "sums": keep.sb("sums", [P, TILES + 2, AW]),
            "row_i": keep.sb("row_i", [P, 1], I32), "row": keep.sb("row", [P, 1]),
        }
        edge_plan(nc, dram, const)
        for layer in range(LAYERS):
            node_phase(nc, dram, const, layer)
            edge_phase(nc, dram, const, layer)
        final_phase(nc, dram, const)



_INS = ["x", "src", "dst", "edge_type_4", "node_type_3", "L0_gnn_W_in", "L0_gnn_b_in", "L0_gnn_Wk", "L0_gnn_bk",
        "L0_gnn_Wq", "L0_gnn_bq", "L0_gnn_Wv", "L0_gnn_bv", "L0_gnn_Wa", "L0_gnn_ba", "L0_gnn_a_rel", "L0_gnn_m_rel",
        "L0_gnn_mu", "L0_gnn_skip"]


def kernel(**inputs):
    import numpy as _np
    import concourse.bacc as _bacc
    from concourse import mybir as _mybir
    from concourse.bass_utils import run_bass_kernel_spmd as _run

    nc = _bacc.Bacc("TRN2", target_bir_lowering=False, num_devices=1)
    arrays, args = {}, {}
    for name in _INS:
        a = _np.ascontiguousarray(inputs[name])
        arrays[f"in_{name}_dram"] = a
        args[name] = nc.dram_tensor(f"in_{name}_dram", a.shape, _mybir.dt.from_np(a.dtype), kind="ExternalInput").ap()
    out = nc.dram_tensor("out_0_dram", (N, D), _mybir.dt.float32, kind="ExternalOutput").ap()
    build_program(nc, args, out)
    r = _run(nc, [arrays], core_ids=[0])
    return r.results[0]["out_0_dram"]
```
